# Optimizing a Trainium2 kernel written in Bass

```python
import numpy as np
import jax
import jax.numpy as jnp

def _softmax(x, axis=-1):
    return jax.nn.softmax(x, axis=axis)

def _gelu(x):
    return jax.nn.gelu(x, approximate=True)

def _silu(x):
    return jax.nn.silu(x)

def _sigmoid(x):
    return jax.nn.sigmoid(x)

def _layernorm(x, axis=-1, eps=1e-05):
    m = jnp.mean(x, axis=axis, keepdims=True)
    v = jnp.var(x, axis=axis, keepdims=True)
    return (x - m) / jnp.sqrt(v + eps)

def _scatter_add(tgt, idx, src, axis=0):
    return tgt.at[idx].add(src)

def _segment_sum(src, seg, n):
    return jax.ops.segment_sum(src, seg, n)
kernel_name = 'mk_lm_tower_d1_tok_ids4096_r4_e9ab71'

def setup_inputs(seed: int=0):
    np.random.seed(seed)
    _w = jnp.asarray

    def _rec_inputs():
        import jax
        import jax.numpy as jnp
        _rk = jax.random.key(seed)
        x = jax.random.randint(jax.random.fold_in(_rk, 1), (16, 1024), 0, 1024, jnp.int32)
        return x
    x = _rec_inputs()

    def _L0_tok_setup():
        import jax, jax.numpy as jnp
        import numpy as np
        BLOCK_SIZE = 16
        VOCAB = 1024
        N_EMBD = 64
        N_EMBD2 = 64
        B, T = (32, 256)

        def _shifted_indices(idx):
            shifts = []
            cur = idx
            for _ in range(BLOCK_SIZE):
                shifts.append(cur)
                cur = jnp.roll(cur, 1, axis=1).at[:, 0].set(VOCAB)
            return jnp.stack(shifts, 0)
        key = jax.random.key(seed)
        k1, k2, k3, k4 = jax.random.split(key, 4)
        idx = jax.random.randint(k1, (B, T), 0, VOCAB)
        wte = jax.random.normal(k2, (VOCAB + 1, N_EMBD), jnp.float32) * 0.02
        fan1 = BLOCK_SIZE * N_EMBD
        w1 = jax.random.normal(k3, (fan1, N_EMBD2), jnp.float32) / np.sqrt(fan1).astype(np.float32)
        b1 = jnp.zeros((N_EMBD2,), jnp.float32)
        w2 = jax.random.normal(k4, (N_EMBD2, VOCAB), jnp.float32) / np.sqrt(N_EMBD2).astype(np.float32)
        b2 = jnp.zeros((VOCAB,), jnp.float32)
        return {'idx': idx, 'wte': wte, 'w1': w1, 'b1': b1, 'w2': w2, 'b2': b2}
    _L0_tok_all = _L0_tok_setup()
    _L0_tok_in = {k: v for k, v in _L0_tok_all.items() if k in ('wte', 'w1', 'b1', 'w2', 'b2')}
    del _L0_tok_all

    def _L0_attn_setup():
        import jax, jax.numpy as jnp
        import numpy as np
        import math
        FACTOR = 1
        key = jax.random.key(seed)
        x = jax.random.normal(key, (8, 128, 1024), dtype=jnp.float32)
        return {'x': x}
    _L0_attn_all = _L0_attn_setup()
    _L0_attn_in = {k: v for k, v in _L0_attn_all.items() if k in ()}
    del _L0_attn_all

    def _L0_ffn_setup():
        import jax, jax.numpy as jnp
        import numpy as np
        key = jax.random.key(seed)
        k = jax.random.split(key, 6)
        x = jax.random.normal(k[0], (4, 512, 1024), jnp.float32)
        W = jax.random.normal(k[1], (1024, 1024), jnp.float32) * 0.02
        bias = jax.random.normal(k[2], (1024,), jnp.float32) * 0.02
        A = jax.random.normal(k[3], (16, 16, 1024), jnp.float32) * 0.02
        Bf = jax.random.normal(k[4], (16, 1024, 16), jnp.float32) * 0.02
        coeffs = jax.random.uniform(k[5], (16,), jnp.float32)
        scales = jnp.full((16,), 0.5, jnp.float32)
        return {'x': x, 'W': W, 'bias': bias, 'A': A, 'Bf': Bf, 'coeffs': coeffs, 'scales': scales}
    _L0_ffn_all = _L0_ffn_setup()
    _L0_ffn_in = {k: v for k, v in _L0_ffn_all.items() if k in ('W', 'bias', 'A', 'Bf', 'coeffs', 'scales')}
    del _L0_ffn_all
    return {'x': x, 'L0_tok_wte': _L0_tok_in['wte'], 'L0_tok_w1': _L0_tok_in['w1'], 'L0_tok_b1': _L0_tok_in['b1'], 'L0_tok_w2': _L0_tok_in['w2'], 'L0_tok_b2': _L0_tok_in['b2'], 'L0_ffn_W': _L0_ffn_in['W'], 'L0_ffn_bias': _L0_ffn_in['bias'], 'L0_ffn_A': _L0_ffn_in['A'], 'L0_ffn_Bf': _L0_ffn_in['Bf'], 'L0_ffn_coeffs': _L0_ffn_in['coeffs'], 'L0_ffn_scales': _L0_ffn_in['scales']}

def reference(x, L0_tok_wte, L0_tok_w1, L0_tok_b1, L0_tok_w2, L0_tok_b2, L0_ffn_W, L0_ffn_bias, L0_ffn_A, L0_ffn_Bf, L0_ffn_coeffs, L0_ffn_scales):
    import jax
    import jax.numpy as jnp

    def _L0_tok_ref(idx, wte, w1, b1, w2, b2):
        import jax, jax.numpy as jnp
        import numpy as np
        BLOCK_SIZE = 16
        VOCAB = 1024
        N_EMBD = 64
        N_EMBD2 = 64
        B, T = (32, 256)

        def _shifted_indices(idx):
            shifts = []
            cur = idx
            for _ in range(BLOCK_SIZE):
                shifts.append(cur)
                cur = jnp.roll(cur, 1, axis=1).at[:, 0].set(VOCAB)
            return jnp.stack(shifts, 0)
        sh = _shifted_indices(idx)
        emb = wte[sh]
        bsz, t = idx.shape
        x = jnp.transpose(emb, (1, 2, 0, 3)).reshape(bsz, t, BLOCK_SIZE * N_EMBD)
        h = jnp.tanh(x @ w1 + b1)
        logits = h @ w2 + b2
        return logits

    def _L0_attn_ref(x):
        import jax, jax.numpy as jnp
        import numpy as np
        import math
        FACTOR = 1
        B, C, L = x.shape
        xh = x[:, None]
        f = jnp.fft.rfft(xh, axis=-1)
        corr = jnp.fft.irfft(f * jnp.conj(f), n=L, axis=-1)
        top_k = int(FACTOR * math.log(L))
        weights, delay = jax.lax.top_k(corr, top_k)
        tmp_corr = jax.nn.softmax(weights, axis=-1)
        init_index = jnp.arange(L)
        idx = (init_index[None, None, None, None, :] + delay[..., None]) % L
        pattern = jnp.take_along_axis(xh[:, :, :, None, :], idx, axis=-1)
        delays_agg = jnp.sum(pattern * tmp_corr[..., None], axis=-2)
        return delays_agg[:, 0]

    def _L0_ffn_ref(x, W, bias, A, Bf, coeffs, scales):
        import jax, jax.numpy as jnp
        import numpy as np
        out = jnp.einsum('bsd,od->bso', x, W) + bias
        xa = jnp.einsum('bsd,erd->ebsr', x, A)
        w = coeffs * scales
        upd = jnp.einsum('ebsr,eor,e->bso', xa, Bf, w)
        return out + upd
    h = _L0_tok_ref(x, L0_tok_wte, L0_tok_w1, L0_tok_b1, L0_tok_w2, L0_tok_b2)
    h = h + _L0_attn_ref(_layernorm(h, axis=-1))
    h = h + _L0_ffn_ref(_layernorm(h, axis=-1), L0_ffn_W, L0_ffn_bias, L0_ffn_A, L0_ffn_Bf, L0_ffn_coeffs, L0_ffn_scales)
    return h

_drawn_inputs = setup_inputs


def setup_inputs(seed=0):
    import zlib

    import numpy as np

    out = dict(_drawn_inputs(seed))
    spreads = {'L0_tok_b1': (0.0, 0.1), 'L0_tok_b2': (0.0, 0.1), 'L0_ffn_scales': (0.5, 0.2)}
    factors = {'L0_ffn_bias': 3.63}
    for name, (base, spread) in spreads.items():
        noise = np.random.default_rng([zlib.crc32(name.encode()), seed]).standard_normal(out[name].shape)
        drawn = base * np.exp(spread * noise) if base else spread * noise
        out[name] = jnp.asarray(drawn.astype(out[name].dtype))
    for name, factor in factors.items():
        out[name] = (out[name] * factor).astype(out[name].dtype)
    return out
```

```python
import numpy as np
import concourse.bass as bass
from concourse import mybir
from concourse.alu_op_type import AluOpType as ALU
from contextlib import ExitStack

F32 = mybir.dt.float32
F32R = mybir.dt.float32r
I32 = mybir.dt.int32
U32 = mybir.dt.uint32
ACT = mybir.ActivationFunctionType
AX = mybir.AxisListType

P = 128
NSEQ, T, L = 16, 1024, 1024
E = 64
J = 16
VOCAB = 1024
NT = T // P
NE, R = 16, 16
ER = NE * R
KC = L // P
HALF = T // 2
EPS = 1e-5
GAP = 112.0
TOPK = 6
PAD = J
SPAN = PAD + T
XW = 32
NX = 8



def ge(eng, sem, count):
    if not isinstance(count, int) or count > 0:
        eng.wait_ge(sem, count)


def wait_alone(eng, sem, count, passed):
    eng.wait_ge(sem, count)
    if not isinstance(count, int):
        eng.sem_inc(passed, 1)


def tower_kernel(nc, ids, wte, w1, b1, w2, b2, wT, bias, aT, bfT, coeffs, scales,
                 ident, stack2, dft, idft, acf, lags, out, force_general=False):
    ctx = ExitStack()
    with ctx:
        def sb(name, shape, dt=F32):
            return ctx.enter_context(nc.sbuf_tensor(name, shape, dt))

        def ps(name, shape):
            return ctx.enter_context(nc.psum_tensor(name, shape, F32))

        def sem(name):
            return ctx.enter_context(nc.semaphore(name))

        split_table = nc.dram_tensor("split_table", (VOCAB + 1, 2 * E), F32, kind="Internal").ap()
        xbar_twice = nc.dram_tensor("xbar_twice", (2 * L,), F32, kind="Internal").ap()

        ids_sb = sb("ids_sb", [P, NSEQ * NT], I32)
        ident_sb = sb("ident_sb", [P, P])
        stack2_sb = sb("stack2_sb", [P, E])
        shift_hi = sb("shift_hi", [P, J, E], F32R)
        shift_lo = sb("shift_lo", [P, J // 2, E], F32R)
        b1_col = sb("b1_col", [E, 1])
        hbar = sb("hbar", [E + 1, P])
        w2c = sb("w2c", [E + 1, L])
        w2mean = sb("w2mean", [E + 1, 1])
        moments = sb("moments", [E + 1, E + 3])
        w_hi = sb("w_hi", [P, L], F32R)
        w_lo = sb("w_lo", [P, L], F32R)
        extra = [sb(f"extra{i}", [P, L], F32R) for i in range(4)]
        aT_sb = sb("aT_sb", [P, KC, ER])
        bfT_sb = sb("bfT_sb", [P, 2, L])
        bias_row = sb("bias_row", [1, L])
        er_w = sb("er_w", [P, 2])
        h_all = sb("h_all", [P, NSEQ * NT * E])

        idx_now = [sb(f"idx_now{p}", [P, NT], I32) for p in range(2)]
        gathered = [sb(f"gathered{p}", [P, NT, 2 * E]) for p in range(2)]
        et_hl = [sb(f"et_hl{p}", [P, SPAN], F32R) for p in range(2)]
        et_hh = [sb(f"et_hh{p}", [P, SPAN + 8], F32R) for p in range(2)]
        ab = [sb(f"ab{p}", [P, T]) for p in range(2)]
        u_hi = [sb(f"u_hi{p}", [P, T], F32R) for p in range(2)]
        u_lo = [sb(f"u_lo{p}", [P, T], F32R) for p in range(2)]
        xT = [sb(f"xT{p}", [P, 2 * P], F32R) for p in range(2)]
        a_sb = [sb(f"a_sb{p}", [P, NT]) for p in range(2)]
        mean_sb = [sb(f"mean_sb{p}", [P, NT]) for p in range(2)]
        u_row = sb("u_row", [P, NT, 2 * E + 1])
        hT = sb("hT", [P, T])
        x_row = sb("x_row", [P, NT, XW], F32R)
        prod = sb("prod", [P, NT, E + 1])
        var = sb("var", [P, NT])
        lin = sb("lin", [P, NT])
        cert = sb("cert", [P, NT])
        cert_max = sb("cert_max", [P, NT])
        var_eps = sb("var_eps", [P, NT])
        inv_std = sb("inv_std", [P, NT])
        a_sq = sb("a_sq", [P, NT])
        var2 = sb("var2", [P, NT])
        var2_eps = sb("var2_eps", [P, NT])
        beta = sb("beta", [P, NT])
        inv_a = sb("inv_a", [P, NT])
        minus_half = sb("minus_half", [P, NT])
        obuf = sb("obuf", [P, 4, 2, L])
        verdict = sb("verdict", [P, 8])
        flag = sb("flag", [1, 1], I32)
        pad_col = sb("pad_col", [E, 1])
        xbar_col = sb("xbar_col", [P, KC])
        g_ones = sb("g_ones", [1, P])
        g_row = sb("g_row", [P, 32])
        g_idx = sb("g_idx", [P, 8], U32)

        g_stats = sb("g_stats", [P, 12])
        g_mv = sb("g_mv", [P, 2])

        wT_sb = h_all[:, :].rearrange("p (c n) -> p c n", c=KC)
        wte_ld = ab[0][:, 0:KC * E].rearrange("p (k e) -> p k e", k=KC)
        last_row = ab[1][0:1, 0:E]
        table_hl = u_hi[0][:, :].rearrange("p (k two e) -> p k two e", k=KC, two=2)
        last_hl = xT[1][0:1, 0:2 * E].rearrange("p (two e) -> p two e", two=2)
        w1_ld = obuf[:, 0, 0, :].rearrange("p (j n) -> p j n", j=J)
        w2cT = obuf[:, 0, 1, 0:KC * (E + 1)].rearrange("p (c n) -> p c n", c=KC)
        xa_sb = obuf[0:E + 1, 1, 0, 0:ER]
        xaT_sb = obuf[:, 1, 0, ER:ER + 2 * (E + 1)].rearrange("p (c n) -> p c n", c=2)
        er_ld = obuf[:, 1, 0, 512:516]
        xbar_row = obuf[0:1, 1, 1, :]
        hankel = obuf[:, 2:4, :, :].rearrange("p a b n -> p (a b n)").rearrange("p (c n) -> p c n", c=KC)

        o_ps = ps("o_ps", [P, 4, 512])
        conv_ps = ps("conv_ps", [P, 512])
        et_ps = ps("et_ps", [P, 512])
        sum_ps = ps("sum_ps", [P, 512])
        mix_ps = ps("mix_ps", [P, 512])

        def y_view(hh):
            return (sum_ps, mix_ps)[hh][:, 0:4 * (E + 3)].rearrange("p (i n) -> p i n", i=4)

        ids_in, table_in, w1_in, consts_in, w2_in, ffn_in, wT_in, hankel_in = (
            sem(n) for n in ("ids_in", "table_in", "w1_in", "consts_in", "w2_in", "ffn_in", "wT_in", "hankel_in"))
        zeros_set = sem("zeros_set")
        table_hi_set = sem("table_hi_set")
        table_split = sem("table_split")
        table_stored = sem("table_stored")
        pads_hi = sem("pads_hi")
        pads_set = sem("pads_set")
        shift_hi_set = sem("shift_hi_set")
        shift_set = sem("shift_set")
        pad_conv_done = sem("pad_conv_done")
        pad_conv_kept = sem("pad_conv_kept")
        w2_sum = sem("w2_sum")
        w2_mean = sem("w2_mean")
        w2_centred = sem("w2_centred")
        w2T_done = sem("w2T_done")
        w2T_kept = sem("w2T_kept")
        hbar_one = sem("hbar_one")
        hbar_set = sem("hbar_set")
        mom_done = sem("mom_done")
        mom_kept = sem("mom_kept")
        xbar_stored = sem("xbar_stored")
        xa_done = sem("xa_done")
        xa_kept = sem("xa_kept")
        g_done = sem("g_done")
        w_hi_set = sem("w_hi_set")
        w_set = sem("w_set")
        row0_in, rows_in = sem("row0_in"), sem("rows_in")
        acf_done = sem("acf_done")
        acf_kept = sem("acf_kept")
        idx_ready = sem("idx_ready")
        rows_gathered = [sem(f"rows_gathered{p}") for p in range(2)]
        et_done = sem("et_done")
        et_kept = sem("et_kept")
        et_top_kept = sem("et_top_kept")
        et_back_kept = sem("et_back_kept")
        conv_done = sem("conv_done")
        ab_a = sem("ab_a")
        ab_b = sem("ab_b")
        sum_done = sem("sum_done")
        h_ready = sem("h_ready")
        h_saved = sem("h_saved")
        ht_done = sem("ht_done")
        ht_kept = sem("ht_kept")
        y_done = sem("y_done")
        prod_ready = sem("prod_ready")
        var_ready = sem("var_ready")
        cert_step = sem("cert_step")
        scal_step = sem("scal_step")
        u_ready = sem("u_ready")
        x_step = sem("x_step")
        x_ready = sem("x_ready")
        ut_done = sem("ut_done")
        hi_kept = sem("hi_kept")
        lo_kept = sem("lo_kept")
        xt_done = sem("xt_done")
        xt_kept = sem("xt_kept")
        o_done = sem("o_done")
        oa_kept = sem("oa_kept")
        ov_kept = sem("ov_kept")
        stored = [sem(f"stored{q}") for q in range(4)]
        v_dve = sem("v_dve")
        v_pool = sem("v_pool")
        flag_set = sem("flag_set")
        g_pe, g_dve, g_act, g_pool = sem("g_pe"), sem("g_dve"), sem("g_act"), sem("g_pool")
        g_link = sem("g_link")
        pool_passed, sp_passed, dve_passed = sem("pool_passed"), sem("sp_passed"), sem("dve_passed")
        g_table_in, g_stored = sem("g_table_in"), sem("g_stored")

        out_pairs = out.rearrange("s (q i p) o -> (s q) p i o", i=2, p=P)
        out_tiles = out.rearrange("s (i p) o -> (s i) p o", p=P)

        FIRST = 4

        def steps(eng, step, between):
            for k in range(FIRST):
                step(k // 2, k % 2, True, k >= 1, k >= 2)
                if k == 0:
                    between()
            with eng.Fori(FIRST // 2, NSEQ // 2) as g:
                step(g, 0, True, True, True)
                step(g, 1, True, True, True)
            for k in range(NSEQ, NSEQ + 2):
                step(k // 2, k % 2, False, k <= NSEQ, True)

        block = ctx.enter_context(nc.Block())

        @block.sync
        def _(sp):
            sp.dma_start(wte_ld, wte[0:VOCAB, :].rearrange("(p k) e -> p k e", k=KC)).then_inc(table_in, 16)
            sp.dma_start(last_row, wte[VOCAB:VOCAB + 1, :]).then_inc(table_in, 16)
            sp.dma_start(pad_col[:, :], wte[VOCAB:VOCAB + 1, :].rearrange("a e -> e a")).then_inc(table_in, 16)
            sp.dma_start(ids_sb[:, :], ids).then_inc(ids_in, 16)
            for half in range(2):
                sp.dma_start(w1_ld[E * half:E * half + E], w1.rearrange("(j e) n -> e j n", e=E)).then_inc(w1_in, 16)
            sp.dma_start(b1_col[:, :], b1).then_inc(w1_in, 16)
            sp.dma_start(ident_sb[:, :], ident).then_inc(consts_in, 16)
            sp.dma_start(stack2_sb[:, :], stack2).then_inc(consts_in, 16)
            sp.dma_start(w2c[0:E, :], w2).then_inc(w2_in, 16)
            sp.dma_start(w2c[E:E + 1, :], b2).then_inc(w2_in, 16)
            sp.wait_ge(table_split, 2)
            sp.dma_start(split_table[0:VOCAB, :].rearrange("(p k) e -> p k e", k=KC),
                         table_hl.bitcast(F32).rearrange("p k two e -> p k (two e)")).then_inc(table_stored, 16)
            sp.dma_start(split_table[VOCAB:VOCAB + 1, :],
                         last_hl.bitcast(F32).rearrange("p two e -> p (two e)")).then_inc(table_stored, 16)
            sp.dma_start(aT_sb[:, :, :], aT.rearrange("(c p) n -> p c n", p=P)).then_inc(ffn_in, 16)
            sp.dma_start(bfT_sb[:, :, :], bfT.rearrange("(c p) n -> p c n", p=P)).then_inc(ffn_in, 16)
            sp.dma_start(er_ld[:, 0:2], coeffs).then_inc(ffn_in, 16)
            sp.dma_start(er_ld[:, 2:4], scales).then_inc(ffn_in, 16)
            sp.dma_start(bias_row[:, :], bias).then_inc(ffn_in, 16)
            sp.dma_start(wT_sb[:, :, :], wT.rearrange("(c p) n -> p c n", p=P)).then_inc(wT_in, 16)
            sp.wait_ge(mom_kept, 5)
            for n in range(2):
                sp.dma_start(xbar_twice[L * n:L * (n + 1)].rearrange("(a n) -> a n", a=1), xbar_row).then_inc(xbar_stored, 16)
            sp.wait_ge(xbar_stored, 32)
            for c in range(KC):
                sp.dma_start(hankel[:, c, :], bass.AP(xbar_twice.tensor, P * c + 1, [[1, P], [1, 512]])).then_inc(hankel_in, 16)
            sp.wait_ge(w_set, 5)
            b_hi, b_lo = u_hi[1][E:E + 1, :], u_lo[1][E:E + 1, :]
            g_hi, g_lo = u_lo[0][E:E + 1, :], u_lo[0][0:1, :]
            bias_hi, bias_lo = u_hi[1][0:1, :], u_lo[1][0:1, :]
            for n, row in enumerate((b_hi, b_lo, g_hi, g_lo, g_hi, bias_hi, bias_lo, bias_hi)):
                sp.dma_start(extra[0][n:n + 1, :].bitcast(F32), row.bitcast(F32)).then_inc(row0_in, 16)
            sp.wait_ge(row0_in, 16 * NX)
            for i in range(1, 4):
                sp.dma_start(extra[i][XW * i:XW * i + NX, :].bitcast(F32), extra[0][0:NX, :].bitcast(F32)).then_inc(rows_in, 16)

            def step(g, u, front, mid, back):
                if back:
                    c = 2 * (g - 1) + u
                    for q in range(4):
                        sp.wait_ge(oa_kept, NT * c + 2 * q + 2)
                        sp.wait_ge(ov_kept, NT * c + 2 * q + 2)
                        sp.dma_start(out_pairs[bass.ds(4 * c + q, 1)].rearrange("a p i o -> (a p) i o"),
                                     obuf[:, q, :, :]).then_inc(stored[q], 16)

            steps(sp, step, lambda: None)
            for q in range(4):
                sp.wait_ge(stored[q], 16 * NSEQ)
            sp.wait_ge(table_stored, 32)

            sp.wait_ge(flag_set, 1)
            need = sp.value_load(flag[0:1, 0:1], min_val=0, max_val=1)
            table = obuf[:, :, :, :].rearrange("p a b n -> p (a b) n")
            with sp.If(need != 0):
                with sp.Fori(0, NSEQ * NT) as t:
                    for n, (src, used, count) in enumerate((
                            (dft, g_dve, 10 * t + 1), (acf, g_pe, 11 * t + 4), (lags, g_pe, 11 * t + 5),
                            (dft, g_dve, 10 * t + 5), (idft, g_pe, 11 * t + 7), (wT, g_pe, 11 * t + 8))):
                        sp.wait_ge(used, count)
                        dst, rows = (table[:, 0, :], src) if n == 2 else (table, src.rearrange("(c p) n -> p c n", p=P))
                        sp.dma_start(dst, rows).then_inc(g_table_in, 16)
                        wait_alone(sp, g_table_in, 96 * t + 16 * n + 16, sp_passed)
                    sp.wait_ge(g_dve, 10 * t + 10)
                    sp.dma_start(out_tiles[bass.ds(t, 1)].rearrange("a p o -> (a p) o"), hT[:, :]).then_inc(g_stored, 16)
                    wait_alone(sp, g_stored, 16 * t + 16, sp_passed)

        @block.gpsimd
        def _(pool):
            for i in range(4):
                pool.memset(extra[i][:, :].bitcast(F32), 0.0)
            pool.memset(x_row[:, :, :].bitcast(F32), 0.0)
            pool.memset(minus_half[:, :], -0.5)
            pool.memset(g_ones[:, :], 1.0)
            pool.memset(cert_max[:, :], -3.0e38)
            pool.memset(u_row[:, :, 2 * E:2 * E + 1], 1.0).then_inc(zeros_set, 1)
            pool.wait_ge(zeros_set, 1)
            pool.memset(x_row[:, :, 0:2].bitcast(F32), 1.0).then_inc(zeros_set, 1)

            def gather(s, p, uses):
                ge(pool, et_done, uses)
                pool.tensor_copy(idx_now[p][:, :], ids_sb[:, bass.ds(NT * s, NT)]).then_inc(idx_ready, 1)
                wait_alone(pool, idx_ready, s + 1, pool_passed)

            def gather_rows(p, i):
                pool.indirect_dma_start(
                    gathered[p][:, i, :], None, split_table,
                    bass.IndirectOffsetOnAxis(ap=idx_now[p][:, i:i + 1].bitcast(U32), axis=0),
                ).then_inc(rows_gathered[p], 16)

            pool.wait_ge(ids_in, 16)
            pool.wait_ge(table_stored, 32)
            gather(0, 0, 0)
            for i in range(NT):
                gather_rows(0, i)

            def step(g, u, front, mid, back, last=False):
                a, b = 2 * g + u, 2 * g + u - 1
                more = front and not last
                if front:
                    for hh in range(2):
                        wait_alone(pool, et_kept, 2 * a + hh + 1, pool_passed)
                        col = PAD + HALF * hh
                        src = et_hl[u][0:E, col:col + HALF].bitcast(F32)
                        pool.tensor_copy(et_hh[u][0:E, col:col + HALF], src).then_inc(et_top_kept, 1)
                if mid:
                    pool.wait_ge(h_ready, b + 1)
                    pool.tensor_copy(h_all[:, bass.ds(NT * E * b, NT * E)].rearrange("p (i e) -> p i e", i=NT),
                                     u_row[:, :, E:2 * E]).then_inc(h_saved, 1)
                if more:
                    gather(a + 1, 1 - u, 2 * a)
                    for i in range(NT // 2):
                        gather_rows(1 - u, i)
                if mid:
                    pb = 1 - u
                    wait_alone(pool, var_ready, 2 * b + 2, pool_passed)
                    pool.tensor_scalar(var_eps[:, :], var[:, :], EPS, None, ALU.add).then_inc(scal_step, 1)
                    wait_alone(pool, scal_step, 7 * b + 1, pool_passed)
                    pool.tensor_tensor(inv_std[:, :], var_eps[:, :], minus_half[:, :], ALU.pow).then_inc(scal_step, 1)
                    wait_alone(pool, scal_step, 7 * b + 2, pool_passed)
                    pool.tensor_scalar(a_sb[pb][:, :], inv_std[:, :], 1.0, None, ALU.add).then_inc(scal_step, 1)
                    wait_alone(pool, scal_step, 7 * b + 3, pool_passed)
                    pool.tensor_tensor(a_sq[:, :], a_sb[pb][:, :], a_sb[pb][:, :], ALU.mult).then_inc(scal_step, 1)
                    wait_alone(pool, scal_step, 7 * b + 4, pool_passed)
                    pool.tensor_tensor(var2[:, :], a_sq[:, :], var[:, :], ALU.mult).then_inc(scal_step, 1)
                    wait_alone(pool, scal_step, 7 * b + 5, pool_passed)
                    pool.tensor_scalar(var2_eps[:, :], var2[:, :], EPS, None, ALU.add).then_inc(scal_step, 1)
                    wait_alone(pool, scal_step, 7 * b + 6, pool_passed)
                    pool.tensor_tensor(beta[:, :], var2_eps[:, :], minus_half[:, :], ALU.pow).then_inc(scal_step, 1)
                if more:
                    for i in range(NT // 2, NT):
                        gather_rows(1 - u, i)

            for k in range(FIRST):
                if k == 1:
                    pool.wait_ge(g_done, 1)
                step(k // 2, k % 2, True, k >= 1, k >= 2)
            with pool.Fori(FIRST // 2, NSEQ // 2 - 1) as g:
                step(g, 0, True, True, True)
                step(g, 1, True, True, True)
            for k in range(NSEQ - 2, NSEQ + 2):
                step(k // 2, k % 2, k < NSEQ, k <= NSEQ, True, last=k == NSEQ - 1)

            pool.wait_ge(v_dve, 1)
            pool.partition_all_reduce(verdict[:, 4:5], verdict[:, 3:4], P, bass.bass_isa.ReduceOp.max).then_inc(v_pool, 1)

            pool.wait_ge(flag_set, 1)
            need = pool.value_load(flag[0:1, 0:1], min_val=0, max_val=1)
            with pool.If(need != 0):
                with pool.Fori(0, NSEQ * NT) as t:
                    for n in range(2):
                        pool.wait_ge(g_dve, 10 * t + (2, 7)[n])
                        pool.tensor_tensor(g_row[:, 4 * n + 1:4 * n + 2], g_row[:, 4 * n:4 * n + 1],
                                           minus_half[:, 0:1], ALU.pow).then_inc(g_pool, 1)

        @block.scalar
        def _(act):
            act.wait_ge(w1_in, 48)
            nc.scalar.activation(hbar[0:E, :], b1_col[:, 0:1].to_broadcast([E, P]), ACT.Tanh).then_inc(hbar_set, 1)
            act.wait_ge(w2T_done, 1)
            for n, bank in enumerate((sum_ps, mix_ps)):
                nc.scalar.copy(w2cT[:, 4 * n:4 * n + 4, :],
                               bank[:, 0:4 * (E + 1)].rearrange("p (c n) -> p c n", c=4)).then_inc(w2T_kept, 1)

            def tile_out(c, pc, i):
                q = i // 2
                if i % 2 == 0:
                    ge(act, stored[q], 16 * c)
                act.wait_ge(o_done, NT * c + i + 1)
                nc.scalar.activation(obuf[:, q, i % 2, 0:512], o_ps[:, 2 * (i % 2), :], ACT.Identity,
                                     bias=mean_sb[pc][:, i:i + 1], scale=a_sb[pc][:, i:i + 1]).then_inc(oa_kept, 1)

            def step(g, u, front, mid, back):
                a, b, c = 2 * g + u, 2 * g + u - 1, 2 * (g - 1) + u
                pb = 1 - u

                def keep_et(hh):
                    act.wait_ge(et_done, 2 * a + hh + 1)
                    col = PAD + HALF * hh
                    nc.scalar.copy(et_hl[u][:, col:col + HALF], et_ps[:, :]).then_inc(et_kept, 1)
                    nc.scalar.copy(et_hh[u][E:P, col + 8:col + 8 + HALF], et_ps[0:E, :]).then_inc(et_back_kept, 1)

                def keep_ht(hh):
                    act.wait_ge(ht_done, 2 * b + hh + 1)
                    nc.scalar.copy(hT[0:E + 1, HALF * hh:HALF * (hh + 1)], mix_ps[0:E + 1, :]).then_inc(ht_kept, 1)

                def keep_a(hh):
                    act.wait_ge(conv_done, 2 * a + hh + 1)
                    nc.scalar.activation(ab[u][0:E, HALF * hh:HALF * (hh + 1)], conv_ps[0:E, :], ACT.Identity,
                                         bias=b1_col[:, 0:1]).then_inc(ab_a, 1)

                if mid:
                    act.wait_ge(sum_done, b + 1)
                    ge(act, h_saved, b)
                    nc.scalar.activation(u_row[:, :, E:2 * E], sum_ps[:, :].rearrange("p (i e) -> p i e", i=NT),
                                         ACT.Tanh).then_inc(h_ready, 1)
                if back:
                    tile_out(c, u, 0)
                if front:
                    keep_et(0)
                if back:
                    tile_out(c, u, 1)
                if mid:
                    keep_ht(0)
                if front:
                    keep_et(1)
                if back:
                    tile_out(c, u, 2)
                if mid:
                    keep_ht(1)
                if back:
                    tile_out(c, u, 3)
                if front:
                    keep_a(0)
                if back:
                    tile_out(c, u, 4)
                    tile_out(c, u, 5)
                if front:
                    keep_a(1)
                if back:
                    tile_out(c, u, 6)
                if mid:
                    for hh, bank in enumerate((sum_ps, mix_ps)):
                        act.wait_ge(ut_done, 2 * b + hh + 1)
                        nc.scalar.copy(u_hi[pb][:, HALF * hh:HALF * (hh + 1)], bank[:, :]).then_inc(hi_kept, 1)
                if back:
                    tile_out(c, u, 7)
                if mid:
                    act.wait_ge(xt_done, b + 1)
                    nc.scalar.copy(xT[pb][:, :], sum_ps[:, 0:2 * P]).then_inc(xt_kept, 1)

            def between():
                act.wait_ge(row0_in, 16 * NX)

            steps(act, step, between)

            act.wait_ge(flag_set, 1)
            need = act.value_load(flag[0:1, 0:1], min_val=0, max_val=1)
            with act.If(need != 0):
                with act.Fori(0, NSEQ * NT) as t:
                    act.wait_ge(g_pe, 11 * t + 1)
                    nc.scalar.copy(hT[0:E + 1, 0:P], mix_ps[0:E + 1, 0:P]).then_inc(g_act, 1)
                    act.wait_ge(g_pe, 11 * t + 3)
                    nc.scalar.copy(ab[1][:, :], o_ps[:, 2:4, :].rearrange("p a n -> p (a n)")).then_inc(g_act, 1)
                    act.wait_ge(g_pe, 11 * t + 4)
                    spec = gathered[0][:, :, :].rearrange("p i n -> p (i n)")
                    nc.scalar.copy(spec, o_ps[:, 0:2, :].rearrange("p a n -> p (a n)"))
                    nc.scalar.activation(gathered[1][:, :, :].rearrange("p i n -> p (i n)"),
                                         o_ps[:, 0:2, :].rearrange("p a n -> p (a n)"), ACT.Square).then_inc(g_act, 1)
                    act.wait_ge(g_dve, 10 * t + 4)
                    nc.scalar.activation(g_row[:, 16:16 + TOPK], g_row[:, 8:8 + TOPK], ACT.Exp, bias=g_row[:, 3:4],
                                         accum_out=g_row[:, 2:3]).then_inc(g_act, 1)
                    act.wait_ge(g_pe, 11 * t + 6)
                    nc.scalar.copy(ab[1][:, :], o_ps[:, 2:4, :].rearrange("p a n -> p (a n)")).then_inc(g_act, 1)
                    act.wait_ge(g_pe, 11 * t + 7)
                    nc.scalar.copy(gathered[1][:, :, :].rearrange("p i n -> p (i n)"),
                                   o_ps[:, 0:2, :].rearrange("p a n -> p (a n)")).then_inc(g_act, 1)
                    act.wait_ge(g_pe, 11 * t + 9)
                    nc.scalar.copy(ab[1][:, :], o_ps[:, 2:4, :].rearrange("p a n -> p (a n)")).then_inc(g_act, 1)

        @block.vector
        def _(dve):
            nc.vector.memset(hbar[E:E + 1, :], 1.0).then_inc(hbar_one, 1)
            dve.wait_ge(table_in, 48)
            nc.vector.tensor_copy(table_hl[:, :, 0, :], wte_ld)
            nc.vector.tensor_copy(last_hl[:, 0, :], last_row)
            for p in range(2):
                nc.vector.tensor_copy(et_hl[p][0:E, 0:PAD], pad_col[:, 0:1].to_broadcast([E, PAD]))
                nc.vector.tensor_copy(et_hh[p][0:E, 0:PAD], pad_col[:, 0:1].to_broadcast([E, PAD]))
                last = nc.vector.tensor_copy(et_hh[p][E:P, 0:PAD + 8], pad_col[:, 0:1].to_broadcast([E, PAD + 8]))
            last.then_inc(table_hi_set, 1)
            dve.wait_ge(table_hi_set, 1)
            nc.vector.tensor_tensor(table_hl[:, :, 1, :], wte_ld, table_hl[:, :, 0, :].bitcast(F32),
                                    ALU.subtract).then_inc(table_split, 1)
            nc.vector.tensor_tensor(last_hl[:, 1, :], last_row, last_hl[:, 0, :].bitcast(F32),
                                    ALU.subtract).then_inc(table_split, 1)
            for p in range(2):
                nc.vector.tensor_tensor(et_hl[p][E:P, 0:PAD], pad_col[:, 0:1].to_broadcast([E, PAD]),
                                        et_hl[p][0:E, 0:PAD].bitcast(F32), ALU.subtract).then_inc(pads_set, 1)
            dve.wait_ge(w1_in, 48)
            nc.vector.tensor_copy(shift_hi[:, :, :], w1_ld).then_inc(shift_hi_set, 1)
            dve.wait_ge(shift_hi_set, 1)
            for half in range(2):
                rows, js = slice(E * half, E * half + E), slice(J // 2 * half, J // 2 * (half + 1))
                nc.vector.tensor_tensor(shift_lo[rows, :, :], w1_ld[rows, js, :], shift_hi[rows, js, :].bitcast(F32),
                                        ALU.subtract).then_inc(shift_set, 1)
            dve.wait_ge(w2_in, 32)
            nc.vector.reduce_sum(w2mean[:, :], w2c[:, :], AX.X).then_inc(w2_sum, 1)
            dve.wait_ge(w2_sum, 1)
            nc.vector.tensor_scalar(w2mean[:, :], w2mean[:, :], 1.0 / L, None, ALU.mult).then_inc(w2_mean, 1)
            dve.wait_ge(w2_mean, 1)
            nc.vector.tensor_scalar(w2c[:, :], w2c[:, :], w2mean[:, 0:1], None, ALU.subtract).then_inc(w2_centred, 1)
            dve.wait_ge(mom_done, 1)
            nc.vector.tensor_copy(moments[:, E + 1:E + 2], w2mean[:, :])
            nc.vector.tensor_scalar(moments[:, 0:E + 1], o_ps[0:E + 1, 0, 0:E + 1], 1.0 / L, None,
                                    ALU.mult).then_inc(mom_kept, 1)
            dve.wait_ge(mom_done, 2)
            nc.vector.tensor_copy(moments[:, E + 2:E + 3], o_ps[0:E + 1, 1, 0:1]).then_inc(mom_kept, 1)
            dve.wait_ge(mom_done, 3)
            nc.vector.tensor_copy(verdict[:, 0:1], o_ps[:, 2, 0:1]).then_inc(mom_kept, 1)
            dve.wait_ge(mom_done, 4)
            nc.vector.tensor_copy(xbar_col[:, :], o_ps[:, 3, 0:KC]).then_inc(mom_kept, 1)
            dve.wait_ge(mom_done, 5)
            nc.vector.tensor_copy(xbar_row, o_ps[0:1, 0:2, :].rearrange("p a n -> p (a n)")).then_inc(mom_kept, 1)

            dve.wait_ge(pad_conv_done, 1)
            for p in range(2):
                nc.vector.tensor_copy(ab[p][E:P, 0:1], conv_ps[E:P, 0:1]).then_inc(pad_conv_kept, 1)

            def tile_out(c, pc, i):
                q = i // 2
                if i % 2 == 0:
                    ge(dve, stored[q], 16 * c)
                dve.wait_ge(o_done, NT * c + i + 1)
                nc.vector.tensor_scalar(obuf[:, q, i % 2, 512:L], o_ps[:, 2 * (i % 2) + 1, :], a_sb[pc][:, i:i + 1],
                                        mean_sb[pc][:, i:i + 1], ALU.mult, ALU.add).then_inc(ov_kept, 1)

            def step(g, u, front, mid, back):
                a, b, c = 2 * g + u, 2 * g + u - 1, 2 * (g - 1) + u
                pb = 1 - u

                def keep_b(hh):
                    dve.wait_ge(conv_done, 2 * a + hh + 1)
                    n = HALF - hh
                    nc.vector.tensor_copy(ab[u][E:P, HALF * hh + 1:HALF * hh + 1 + n], conv_ps[E:P, 0:n]).then_inc(ab_b, 1)

                if back:
                    for i in range(4):
                        tile_out(c, u, i)
                if mid:
                    for hh in range(2):
                        tiles = slice(4 * hh, 4 * hh + 4)
                        dve.wait_ge(y_done, 2 * b + hh + 1)
                        y = y_view(hh)
                        nc.vector.tensor_tensor(prod[:, tiles, :], y[:, :, 0:E + 1], u_row[:, tiles, E:2 * E + 1],
                                                ALU.mult).then_inc(prod_ready, 1)
                        nc.vector.tensor_copy(mean_sb[pb][:, tiles], y[:, :, E + 1])
                        nc.vector.tensor_copy(lin[:, tiles], y[:, :, E + 2])
                        dve.wait_ge(prod_ready, 2 * b + hh + 1)
                        nc.vector.tensor_reduce(var[:, tiles], prod[:, tiles, :], AX.X, ALU.add).then_inc(var_ready, 1)
                    dve.wait_ge(var_ready, 2 * b + 2)
                    nc.vector.tensor_scalar(cert[:, :], var[:, :], 2 * GAP + 4 * L, None, ALU.mult).then_inc(cert_step, 1)
                    dve.wait_ge(cert_step, 3 * b + 1)
                    nc.vector.scalar_tensor_tensor(cert[:, :], lin[:, :], -8.0 * L, cert[:, :], ALU.mult,
                                                   ALU.add).then_inc(cert_step, 1)
                    dve.wait_ge(cert_step, 3 * b + 2)
                    nc.vector.tensor_tensor(cert_max[:, :], cert_max[:, :], cert[:, :], ALU.max).then_inc(cert_step, 1)
                if front:
                    keep_b(0)
                if back:
                    tile_out(c, u, 4)
                    tile_out(c, u, 5)
                if mid:
                    dve.wait_ge(scal_step, 7 * b + 7)
                    nc.vector.tensor_tensor(u_row[:, :, 0:E], u_row[:, :, E:2 * E],
                                            beta[:, :].unsqueeze(2).to_broadcast([P, NT, E]), ALU.mult).then_inc(u_ready, 1)
                    nc.vector.reciprocal(inv_a[:, :], a_sb[pb][:, :]).then_inc(x_step, 1)
                    nc.vector.tensor_copy(x_row[:, :, 2:4], beta[:, :].unsqueeze(2).to_broadcast([P, NT, 2])).then_inc(x_step, 1)
                    dve.wait_ge(x_step, 3 * b + 1)
                    nc.vector.tensor_copy(x_row[:, :, 5:7], inv_a[:, :].unsqueeze(2).to_broadcast([P, NT, 2])).then_inc(x_step, 1)
                    dve.wait_ge(x_step, 3 * b + 2)
                    nc.vector.tensor_tensor(x_row[:, :, 4], beta[:, :], x_row[:, :, 2].bitcast(F32), ALU.subtract)
                    dve.wait_ge(x_step, 3 * b + 3)
                    nc.vector.tensor_tensor(x_row[:, :, 7], inv_a[:, :], x_row[:, :, 5].bitcast(F32),
                                            ALU.subtract).then_inc(x_ready, 1)
                if front:
                    keep_b(1)
                if back:
                    tile_out(c, u, 6)
                if mid:
                    for hh, bank in enumerate((sum_ps, mix_ps)):
                        dve.wait_ge(hi_kept, 2 * b + hh + 1)
                        cols = slice(HALF * hh, HALF * (hh + 1))
                        nc.vector.tensor_tensor(u_lo[pb][:, cols], bank[:, :], u_hi[pb][:, cols].bitcast(F32),
                                                ALU.subtract).then_inc(lo_kept, 1)
                if back:
                    tile_out(c, u, 7)

            def between():
                dve.wait_ge(ffn_in, 80)
                nc.vector.tensor_tensor(er_w[:, :], er_ld[:, 0:2], er_ld[:, 2:4], ALU.mult).then_inc(xa_kept, 1)
                dve.wait_ge(xa_done, 1)
                nc.vector.tensor_copy(xa_sb, sum_ps[0:E + 1, 0:ER]).then_inc(xa_kept, 1)
                dve.wait_ge(xa_done, 2)
                for n in range(2):
                    nc.vector.tensor_scalar(xaT_sb[:, n, :], mix_ps[:, (E + 1) * n:(E + 1) * (n + 1)], er_w[:, n:n + 1],
                                            None, ALU.mult).then_inc(xa_kept, 1)
                dve.wait_ge(table_stored, 32)
                nc.vector.tensor_copy(w_hi[E:P, :], w2c[0:E, :])
                nc.vector.tensor_copy(u_hi[1][0:E + 1, :], w2c[:, :]).then_inc(w_hi_set, 1)
                dve.wait_ge(w_hi_set, 1)
                nc.vector.tensor_tensor(w_lo[E:P, :], w2c[0:E, :], u_hi[1][0:E, :].bitcast(F32), ALU.subtract).then_inc(w_set, 1)
                nc.vector.tensor_tensor(u_lo[1][E:E + 1, :], w2c[E:E + 1, :], u_hi[1][E:E + 1, :].bitcast(F32),
                                        ALU.subtract).then_inc(w_set, 1)
                dve.wait_ge(w_set, 2)
                nc.vector.tensor_copy(u_hi[1][0:1, :], bias_row[:, :]).then_inc(w_hi_set, 1)
                dve.wait_ge(w_hi_set, 2)
                nc.vector.tensor_tensor(u_lo[1][0:1, :], bias_row[:, :], u_hi[1][0:1, :].bitcast(F32),
                                        ALU.subtract).then_inc(w_set, 1)
                dve.wait_ge(g_done, 1)
                gw = o_ps[0:E, 0:2, :].rearrange("p a n -> p (a n)")
                gb = o_ps[E:E + 1, 0:2, :].rearrange("p a n -> p (a n)")
                nc.vector.tensor_copy(u_lo[0][E:E + 1, :], gb).then_inc(w_hi_set, 1)
                nc.vector.tensor_copy(w_hi[0:E, :], gw).then_inc(w_hi_set, 1)
                dve.wait_ge(w_hi_set, 3)
                nc.vector.tensor_tensor(u_lo[0][0:1, :], gb, u_lo[0][E:E + 1, :].bitcast(F32), ALU.subtract).then_inc(w_set, 1)
                dve.wait_ge(w_hi_set, 4)
                nc.vector.tensor_tensor(w_lo[0:E, :], gw, w_hi[0:E, :].bitcast(F32), ALU.subtract).then_inc(w_set, 1)
                dve.wait_ge(acf_done, 1)
                nc.vector.reduce_max(verdict[0:1, 1:2], o_ps[0:1, 2, :], AX.X).then_inc(acf_kept, 1)
                dve.wait_ge(acf_kept, 1)
                nc.vector.tensor_tensor(verdict[0:1, 2:3], o_ps[0:1, 3, 0:1], verdict[0:1, 1:2],
                                        ALU.subtract).then_inc(acf_kept, 1)
                dve.wait_ge(row0_in, 16 * NX)

            steps(dve, step, between)

            dve.wait_ge(cert_step, 3 * NSEQ)
            nc.vector.reduce_max(verdict[:, 3:4], cert_max[:, :], AX.X).then_inc(v_dve, 1)
            dve.wait_ge(v_pool, 1)
            nc.vector.scalar_tensor_tensor(verdict[0:1, 5:6], verdict[0:1, 0:1], 4.0 * L, verdict[0:1, 4:5], ALU.mult,
                                           ALU.add).then_inc(v_dve, 1)
            dve.wait_ge(v_dve, 2)
            nc.vector.tensor_scalar(verdict[0:1, 6:7], verdict[0:1, 2:3], 0.98, -2 * GAP * EPS, ALU.mult,
                                    ALU.add).then_inc(v_dve, 1)
            dve.wait_ge(v_dve, 3)
            nc.vector.tensor_tensor(verdict[0:1, 7:8], verdict[0:1, 5:6], verdict[0:1, 6:7], ALU.is_le).then_inc(v_dve, 1)
            dve.wait_ge(v_dve, 4)
            scale, shift = (0.0, 1.0) if force_general else (-1.0, 1.0)
            nc.vector.tensor_scalar(flag[:, :], verdict[0:1, 7:8], scale, shift, ALU.mult, ALU.add).then_inc(flag_set, 1)

            dve.wait_ge(flag_set, 1)
            need = dve.value_load(flag[0:1, 0:1], min_val=0, max_val=1)
            with dve.If(need != 0):
                ab0, ab1 = ab[0][:, :], ab[1][:, :]
                rows = u_row[:, :, :].rearrange("p i n -> p (i n)")[:, 0:L]
                spec_x, spec_w = (gathered[n][:, :, :].rearrange("p i n -> p (i n)") for n in range(2))
                left, right = (o_ps[:, n:n + 2, :].rearrange("p a n -> p (a n)") for n in (0, 2))
                lag_row = obuf[:, 0, 0, :]
                LINKS = 26
                with dve.Fori(0, NSEQ * NT) as t:
                    count = [0]

                    def link(ins):
                        count[0] += 1
                        ins.then_inc(g_link, 1)
                        wait_alone(dve, g_link, LINKS * t + count[0], dve_passed)

                    def variance_eps(src, col):
                        for n in range(2):
                            last = nc.vector.bn_stats(g_stats[:, 6 * n:6 * n + 6], src[:, 512 * n:512 * (n + 1)])
                        link(last)
                        link(nc.vector.bn_aggr(g_mv[:, :], g_stats[:, :]))
                        nc.vector.tensor_scalar(g_row[:, col:col + 1], g_mv[:, 1:2], EPS, None, ALU.add).then_inc(g_dve, 1)

                    link(nc.vector.tensor_copy(prod[:, 0, 0:E], h_all[:, bass.ds(E * t, E)]))
                    nc.vector.memset(prod[:, 0, E:E + 1], 1.0).then_inc(g_dve, 1)
                    dve.wait_ge(g_pe, 11 * t + 2)
                    variance_eps(left, 0)
                    link(nc.vector.tensor_copy(g_row[:, 6:7], sum_ps[:, 0:1]))
                    link(nc.vector.tensor_scalar(rows, left, g_row[:, 6:7], None, ALU.add))
                    dve.wait_ge(g_pool, 2 * t + 1)
                    nc.vector.tensor_scalar(ab0, left, g_mv[:, 0:1], g_row[:, 1:2], ALU.subtract, ALU.mult).then_inc(g_dve, 1)
                    dve.wait_ge(g_pe, 11 * t + 5)
                    link(nc.vector.tensor_copy(ab0, right))
                    link(nc.vector.max(g_row[:, 8:16], ab0))
                    link(nc.vector.max_index(g_idx[:, :], g_row[:, 8:16], ab0))
                    nc.vector.tensor_copy(g_row[:, 24:32], g_idx[:, :])
                    link(nc.vector.tensor_scalar(g_row[:, 3:4], g_row[:, 8:9], -1.0, None, ALU.mult))
                    nc.vector.tensor_scalar(g_row[:, 7:8], g_row[:, 8:9], -1.0, None, ALU.mult).then_inc(g_dve, 1)
                    dve.wait_ge(g_act, 7 * t + 4)
                    link(nc.vector.reciprocal(g_row[:, 2:3], g_row[:, 2:3]))
                    link(nc.vector.tensor_scalar(g_row[:, 16:16 + TOPK], g_row[:, 16:16 + TOPK], g_row[:, 2:3], None, ALU.mult))
                    dve.wait_ge(g_table_in, 96 * t + 48)
                    link(nc.vector.tensor_scalar(ab0, lag_row, g_row[:, 24:25], g_row[:, 16:17], ALU.is_equal, ALU.mult))
                    for n in range(1, TOPK):
                        link(nc.vector.tensor_scalar(left, lag_row, g_row[:, 24 + n:25 + n], g_row[:, 16 + n:17 + n],
                                                     ALU.is_equal, ALU.mult))
                        add = nc.vector.tensor_tensor(ab0, ab0, left, ALU.add)
                        if n < TOPK - 1:
                            link(add)
                    add.then_inc(g_dve, 1)
                    dve.wait_ge(g_act, 7 * t + 6)
                    h_ = L // 2
                    xc, xs, wc, ws = spec_x[:, 0:h_], spec_x[:, h_:L], spec_w[:, 0:h_], spec_w[:, h_:L]
                    nc.vector.tensor_tensor(ab0[:, 0:h_], xc, wc, ALU.mult)
                    nc.vector.tensor_tensor(ab0[:, h_:L], xs, wc, ALU.mult)
                    nc.vector.tensor_tensor(left[:, 0:h_], xs, ws, ALU.mult)
                    link(nc.vector.tensor_tensor(left[:, h_:L], xc, ws, ALU.mult))
                    nc.vector.tensor_tensor(ab0[:, 0:h_], ab0[:, 0:h_], left[:, 0:h_], ALU.add)
                    link(nc.vector.tensor_tensor(ab0[:, h_:L], ab0[:, h_:L], left[:, h_:L], ALU.subtract))
                    nc.vector.tensor_tensor(ab0[0:1, 0:P], xc[0:1, 0:P], wc[0:1, 0:P], ALU.mult)
                    nc.vector.tensor_tensor(ab0[0:1, h_:h_ + P], xs[0:1, 0:P], ws[0:1, 0:P], ALU.mult).then_inc(g_dve, 1)
                    dve.wait_ge(g_pe, 11 * t + 8)
                    link(nc.vector.tensor_tensor(rows, rows, left, ALU.add))
                    variance_eps(rows, 4)
                    dve.wait_ge(g_pool, 2 * t + 2)
                    nc.vector.tensor_scalar(ab0, rows, g_mv[:, 0:1], g_row[:, 5:6], ALU.subtract, ALU.mult).then_inc(g_dve, 1)
                    dve.wait_ge(g_pe, 11 * t + 10)
                    for n in range(2):
                        last = nc.vector.tensor_scalar(spec_w[:, P * n:P * (n + 1)], sum_ps[:, P * n:P * (n + 1)],
                                                       er_w[:, n:n + 1], None, ALU.mult)
                    last.then_inc(g_dve, 1)
                    dve.wait_ge(g_pe, 11 * t + 11)
                    nc.vector.tensor_tensor(hT[:, :], rows, left, ALU.add).then_inc(g_dve, 1)
                    dve.wait_ge(g_stored, 16 * t + 16)
                    assert count[0] == LINKS, count


        @block.tensor
        def _(pe):
            mm, tr = nc.tensor.matmul, nc.tensor.transpose

            pe.wait_ge(consts_in, 32)
            pe.wait_ge(w2_centred, 1)
            for c in range(KC):
                bank = (sum_ps, mix_ps)[c // 4]
                last = tr(bank[:, (E + 1) * (c % 4):(E + 1) * (c % 4 + 1)], w2c[:, P * c:P * (c + 1)], ident_sb[0:E + 1, 0:E + 1])
            last.then_inc(w2T_done, 1)
            pe.wait_ge(w2T_kept, 2)
            for c in range(KC):
                last = mm(o_ps[0:E + 1, 0, 0:E + 1], w2cT[:, c, :], w2cT[:, c, :], start=(c == 0), stop=(c == KC - 1))
            last.then_inc(mom_done, 1)
            pe.wait_ge(mom_kept, 1)
            pe.wait_ge(hbar_set, 1)
            pe.wait_ge(hbar_one, 1)
            mm(o_ps[0:E + 1, 1, 0:1], moments[:, 0:E + 1], hbar[:, 0:1], start=True, stop=True).then_inc(mom_done, 1)
            pe.wait_ge(mom_kept, 2)
            mm(o_ps[:, 2, 0:1], hbar[:, :], moments[:, E + 2:E + 3], start=True, stop=True).then_inc(mom_done, 1)
            for c in range(KC):
                last = mm(o_ps[:, 3, c:c + 1], w2c[:, P * c:P * (c + 1)], hbar[:, 0:1], start=True, stop=True)
            last.then_inc(mom_done, 1)
            for n in range(2):
                last = mm(o_ps[0:1, n, :], hbar[:, 0:1], w2c[:, 512 * n:512 * (n + 1)], start=True, stop=True)
            last.then_inc(mom_done, 1)

            def conv(u, col, width):
                for m in range(J // 2):
                    mm(conv_ps[:, 0:width], shift_hi[:, 2 * m:2 * m + 2, :], et_hl[u][:, col - 2 * m:col - 2 * m + width],
                       start=(m == 0), stop=False)
                for m in range(J // 4):
                    last = mm(conv_ps[:, 0:width], shift_lo[:, 2 * m:2 * m + 2, :],
                              et_hh[u][:, col - 2 * m:col - 2 * m + width], start=False, stop=(m == J // 4 - 1))
                return last

            pe.wait_ge(shift_set, 2)
            pe.wait_ge(pads_set, 2)
            conv(0, J - 2, 2).then_inc(pad_conv_done, 1)
            pe.wait_ge(pad_conv_kept, 2)

            def step(g, u, front, mid, back):
                a, b, c = 2 * g + u, 2 * g + u - 1, 2 * (g - 1) + u
                pb = 1 - u

                def tile_product(i):
                    if i == 0:
                        pe.wait_ge(hi_kept, 2 * c + 2)
                        pe.wait_ge(lo_kept, 2 * c + 2)
                        pe.wait_ge(xt_kept, c + 1)
                    ge(pe, oa_kept, NT * c + i - 1)
                    ge(pe, ov_kept, NT * c + i - 1)
                    cols = slice(P * i, P * (i + 1))
                    factors = ((u_hi[u][:, cols], w_hi), (u_lo[u][:, cols], w_hi), (u_hi[u][:, cols], w_lo),
                               (xT[u][:, P * (i // 4):P * (i // 4 + 1)], extra[i % 4]))
                    for n in range(2):
                        for f, (lhsT, rhs) in enumerate(factors):
                            last = mm(o_ps[:, 2 * (i % 2) + n, :], lhsT, rhs[:, 512 * n:512 * (n + 1)],
                                      start=(f == 0), stop=(f == len(factors) - 1))
                    last.then_inc(o_done, 1)

                def transpose_rows(hh):
                    if hh == 0:
                        pe.wait_ge(rows_gathered[u], 16 * NT * (g + 1))
                    ge(pe, et_back_kept, 2 * a + hh)
                    for i in range(4):
                        last = tr(et_ps[:, P * i:P * (i + 1)], gathered[u][:, 4 * hh + i, :], ident_sb[:, :])
                    last.then_inc(et_done, 1)

                def transpose_h(hh):
                    if hh == 0:
                        pe.wait_ge(h_ready, b + 1)
                        ge(pe, hi_kept, 2 * b)
                        ge(pe, lo_kept, 2 * b)
                    else:
                        pe.wait_ge(ht_kept, 2 * b + 1)
                    for i in range(4):
                        last = tr(mix_ps[0:E + 1, P * i:P * (i + 1)], u_row[:, 4 * hh + i, E:2 * E + 1], ident_sb[:, :])
                    last.then_inc(ht_done, 1)

                def moments_of(hh):
                    pe.wait_ge(ht_kept, 2 * b + hh + 1)
                    y = y_view(hh)
                    for i in range(4):
                        col = HALF * hh + P * i
                        last = mm(y[:, i, :], hT[0:E + 1, col:col + P], moments[:, :], start=True, stop=True)
                    last.then_inc(y_done, 1)

                def conv_half(hh):
                    pe.wait_ge(et_kept, 2 * a + hh + 1)
                    pe.wait_ge(et_top_kept, 2 * a + hh + 1)
                    pe.wait_ge(et_back_kept, 2 * a + hh + 1)
                    ge(pe, ab_a, 2 * a + hh)
                    ge(pe, ab_b, 2 * a + hh)
                    conv(u, PAD + HALF * hh, HALF).then_inc(conv_done, 1)

                if mid:
                    pe.wait_ge(ab_a, 2 * b + 2)
                    pe.wait_ge(ab_b, 2 * b + 2)
                    ge(pe, xt_kept, b)
                    for i in range(NT):
                        last = mm(sum_ps[:, E * i:E * (i + 1)], ab[pb][:, P * i:P * (i + 1)], stack2_sb[:, :],
                                  start=True, stop=True)
                    last.then_inc(sum_done, 1)
                if back:
                    tile_product(0)
                if front:
                    transpose_rows(0)
                if back:
                    tile_product(1)
                if mid:
                    transpose_h(0)
                if front:
                    transpose_rows(1)
                if back:
                    tile_product(2)
                if mid:
                    transpose_h(1)
                if back:
                    tile_product(3)
                if mid:
                    moments_of(0)
                    moments_of(1)
                if front:
                    conv_half(0)
                if back:
                    tile_product(4)
                    tile_product(5)
                if front:
                    conv_half(1)
                if back:
                    tile_product(6)
                if mid:
                    pe.wait_ge(u_ready, b + 1)
                    for hh, bank in enumerate((sum_ps, mix_ps)):
                        for i in range(4):
                            last = tr(bank[:, P * i:P * (i + 1)], u_row[:, 4 * hh + i, 0:2 * E], ident_sb[:, :])
                        last.then_inc(ut_done, 1)
                if back:
                    tile_product(7)
                if mid:
                    pe.wait_ge(x_ready, b + 1)
                    pe.wait_ge(hi_kept, 2 * b + 1)
                    pe.wait_ge(lo_kept, 2 * b + 1)
                    for hh in range(2):
                        last = tr(sum_ps[:, P * hh:P * (hh + 1)], x_row[:, 4 * hh:4 * hh + 4, :].bitcast(F32).rearrange("p i x -> p (i x)"),
                                  ident_sb[:, :])
                    last.then_inc(xt_done, 1)

            def between():
                pe.wait_ge(ffn_in, 80)
                for c in range(KC):
                    last = mm(sum_ps[0:E + 1, 0:ER], w2cT[:, c, :], aT_sb[:, c, :], start=(c == 0), stop=(c == KC - 1))
                last.then_inc(xa_done, 1)
                pe.wait_ge(mom_kept, 5)
                pe.wait_ge(wT_in, 16)
                for c in range(KC):
                    for n in range(2):
                        mm(o_ps[0:E + 1, n, :], w2cT[:, c, :], wT_sb[:, c, 512 * n:512 * (n + 1)], start=(c == 0), stop=False)
                pe.wait_ge(xa_kept, 2)
                for n in range(2):
                    last = tr(mix_ps[:, (E + 1) * n:(E + 1) * (n + 1)], xa_sb[:, P * n:P * (n + 1)], ident_sb[0:E + 1, 0:E + 1])
                last.then_inc(xa_done, 1)
                pe.wait_ge(xa_kept, 4)
                for e in range(2):
                    for n in range(2):
                        last = mm(o_ps[0:E + 1, n, :], xaT_sb[:, e, :], bfT_sb[:, e, 512 * n:512 * (n + 1)], start=False, stop=(e == 1))
                last.then_inc(g_done, 1)
                pe.wait_ge(hankel_in, 16 * KC)
                for c in range(KC):
                    mm(o_ps[0:1, 2, :], xbar_col[:, c:c + 1], hankel[:, c, :], start=(c == 0), stop=(c == KC - 1))
                for c in range(KC):
                    last = mm(o_ps[0:1, 3, 0:1], xbar_col[:, c:c + 1], xbar_col[:, c:c + 1], start=(c == 0), stop=(c == KC - 1))
                last.then_inc(acf_done, 1)
                pe.wait_ge(w_set, 5)
                pe.wait_ge(acf_kept, 2)
                pe.wait_ge(rows_in, 48)

            steps(pe, step, between)

            pe.wait_ge(flag_set, 1)
            need = pe.value_load(flag[0:1, 0:1], min_val=0, max_val=1)
            with pe.If(need != 0):
                ab0, ab1 = ab[0][:, :], ab[1][:, :]
                spec_w = gathered[1][:, :, :].rearrange("p i n -> p (i n)")
                left, right = (o_ps[:, n:n + 2, :].rearrange("p a n -> p (a n)") for n in (0, 2))
                table = obuf[:, :, :, :].rearrange("p a b n -> p (a b) n")

                def transpose_all():
                    for c in range(KC):
                        last = tr(right[:, P * c:P * (c + 1)], ab0[:, P * c:P * (c + 1)], ident_sb[:, :])
                    last.then_inc(g_pe, 1)

                def spectrum():
                    for m in range(KC):
                        for c in range(KC):
                            last = mm(left[:, P * m:P * (m + 1)], table[:, c, P * m:P * (m + 1)], ab1[:, P * c:P * (c + 1)],
                                      start=(c == 0), stop=(c == KC - 1))
                    last.then_inc(g_pe, 1)

                def rows_from(dst, lhsT):
                    for n in range(2):
                        for c in range(KC):
                            last = mm(dst[:, 512 * n:512 * (n + 1)], lhsT[:, P * c:P * (c + 1)], table[:, c, 512 * n:512 * (n + 1)],
                                      start=(c == 0), stop=(c == KC - 1))
                    last.then_inc(g_pe, 1)

                with pe.Fori(0, NSEQ * NT) as t:
                    pe.wait_ge(g_dve, 10 * t + 1)
                    tr(mix_ps[0:E + 1, 0:P], prod[:, 0, :], ident_sb[:, :]).then_inc(g_pe, 1)
                    pe.wait_ge(g_act, 7 * t + 1)
                    for n in range(2):
                        mm(left[:, 512 * n:512 * (n + 1)], hT[0:E + 1, 0:P], w2c[:, 512 * n:512 * (n + 1)], start=True, stop=True)
                    mm(sum_ps[:, 0:1], hT[0:E + 1, 0:P], w2mean[:, :], start=True, stop=True).then_inc(g_pe, 1)
                    pe.wait_ge(g_dve, 10 * t + 3)
                    transpose_all()
                    pe.wait_ge(g_act, 7 * t + 2)
                    pe.wait_ge(g_table_in, 96 * t + 16)
                    spectrum()
                    pe.wait_ge(g_act, 7 * t + 3)
                    pe.wait_ge(g_table_in, 96 * t + 32)
                    rows_from(right, spec_w)
                    pe.wait_ge(g_dve, 10 * t + 5)
                    transpose_all()
                    pe.wait_ge(g_act, 7 * t + 5)
                    pe.wait_ge(g_table_in, 96 * t + 64)
                    spectrum()
                    pe.wait_ge(g_dve, 10 * t + 6)
                    pe.wait_ge(g_table_in, 96 * t + 80)
                    rows_from(left, ab0)
                    pe.wait_ge(g_dve, 10 * t + 8)
                    transpose_all()
                    pe.wait_ge(g_act, 7 * t + 7)
                    for e in range(2):
                        for c in range(KC):
                            last = mm(sum_ps[:, P * e:P * (e + 1)], aT_sb[:, c, P * e:P * (e + 1)], ab1[:, P * c:P * (c + 1)],
                                      start=(c == 0), stop=(c == KC - 1))
                    last.then_inc(g_pe, 1)
                    pe.wait_ge(g_dve, 10 * t + 9)
                    pe.wait_ge(g_table_in, 96 * t + 96)
                    for n in range(2):
                        cols = slice(512 * n, 512 * (n + 1))
                        for c in range(KC):
                            mm(left[:, cols], ab1[:, P * c:P * (c + 1)], table[:, c, cols], start=(c == 0), stop=False)
                        for e in range(2):
                            mm(left[:, cols], spec_w[:, P * e:P * (e + 1)], bfT_sb[:, e, cols], start=False, stop=False)
                        last = mm(left[:, cols], g_ones[:, :], bias_row[:, cols], start=False, stop=True)
                    last.then_inc(g_pe, 1)



def kernel(**inputs):
    import concourse.bacc as bacc
    from concourse.bass_utils import run_bass_kernel_spmd

    x, w = inputs["x"], inputs["L0_ffn_W"]
    a, bf = inputs["L0_ffn_A"], inputs["L0_ffn_Bf"]
    by_rank = lambda v: np.ascontiguousarray(np.repeat(v, R).reshape(2, P).T)
    half = L // 2
    freq = np.concatenate([np.arange(half), np.arange(half)])
    freq[half] = half
    turn = np.outer(np.arange(L), freq) % L
    cosine = np.cos(2 * np.pi * np.minimum(turn, L - turn) / L)
    sine = np.sin(2 * np.pi * turn / L)
    dft = np.concatenate([cosine[:, :half + 1], sine[:, half + 1:]], 1)
    weight = np.where((np.arange(L) == 0) | (np.arange(L) == half), 1.0, 2.0) / L
    arrays = {
        "ids": np.ascontiguousarray(np.asarray(x).reshape(NSEQ * NT, P).T),
        "wte": inputs["L0_tok_wte"], "w1": inputs["L0_tok_w1"], "b1": inputs["L0_tok_b1"].reshape(E, 1),
        "w2": inputs["L0_tok_w2"], "b2": inputs["L0_tok_b2"].reshape(1, L),
        "wT": np.ascontiguousarray(w.T), "bias": inputs["L0_ffn_bias"].reshape(1, L),
        "aT": np.ascontiguousarray(a.reshape(ER, L).T),
        "bfT": np.ascontiguousarray(bf.transpose(0, 2, 1).reshape(ER, L)),
        "coeffs": by_rank(inputs["L0_ffn_coeffs"]), "scales": by_rank(inputs["L0_ffn_scales"]),
        "ident": np.eye(P, dtype=np.float32), "stack2": np.tile(np.eye(E, dtype=np.float32), (2, 1)),
        "dft": dft.astype(np.float32),
        "idft": np.ascontiguousarray((dft * weight).T.astype(np.float32)),
        "acf": np.ascontiguousarray((cosine * weight).T.astype(np.float32)),
        "lags": np.tile(np.arange(L, dtype=np.float32), (P, 1)),
    }
    arrays = {n: np.ascontiguousarray(v) for n, v in arrays.items()}
    nc = bacc.Bacc("TRN2", target_bir_lowering=False, num_devices=1)
    args = {n: nc.dram_tensor(f"in_{n}", v.shape, mybir.dt.from_np(v.dtype), kind="ExternalInput").ap()
            for n, v in arrays.items()}
    out = nc.dram_tensor("out", (NSEQ, T, L), F32, kind="ExternalOutput").ap()
    tower_kernel(nc, out=out, **args)
    res = run_bass_kernel_spmd(nc, [{f"in_{n}": v for n, v in arrays.items()}], core_ids=[0])
    return res.results[0]["out"]
```

```python
import numpy as np
import concourse.bass as bass
from concourse import mybir
from concourse.alu_op_type import AluOpType as ALU
from contextlib import ExitStack

F32 = mybir.dt.float32
F32R = mybir.dt.float32r
I32 = mybir.dt.int32
U32 = mybir.dt.uint32
ACT = mybir.ActivationFunctionType
AX = mybir.AxisListType

P = 128
NSEQ, T, L = 16, 1024, 1024
E = 64
J = 16
VOCAB = 1024
NT = T // P
NE, R = 16, 16
ER = NE * R
KC = L // P
HALF = T // 2
EPS = 1e-5
GAP = 112.0
TOPK = 6
PAD = J
SPAN = PAD + T
XW = 32
NX = 8



def ge(eng, sem, count):
    if not isinstance(count, int) or count > 0:
        eng.wait_ge(sem, count)


def wait_alone(eng, sem, count, passed):
    eng.wait_ge(sem, count)
    if not isinstance(count, int):
        eng.sem_inc(passed, 1)


def tower_kernel(nc, ids, wte, w1, b1, w2, b2, wT, bias, aT, bfT, coeffs, scales,
                 ident, dft, idft, acf, lags, out, force_general=False):
    ctx = ExitStack()
    with ctx:
        def sb(name, shape, dt=F32):
            return ctx.enter_context(nc.sbuf_tensor(name, shape, dt))

        def ps(name, shape):
            return ctx.enter_context(nc.psum_tensor(name, shape, F32))

        def sem(name):
            return ctx.enter_context(nc.semaphore(name))

        split_table = nc.dram_tensor("split_table", (VOCAB + 1, 2 * E), F32, kind="Internal").ap()
        xbar_twice = nc.dram_tensor("xbar_twice", (2 * L,), F32, kind="Internal").ap()

        ids_sb = sb("ids_sb", [P, NSEQ * NT], I32)
        ident_sb = sb("ident_sb", [P, P])
        shift_hi = sb("shift_hi", [P, J, E], F32R)
        shift_lo = sb("shift_lo", [P, J // 2, E], F32R)
        b1_col = sb("b1_col", [E, 1])
        hbar = sb("hbar", [E + 1, P])
        w2c = sb("w2c", [E + 1, L])
        w2mean = sb("w2mean", [E + 1, 1])
        moments = sb("moments", [E + 1, E + 3])
        w_hi = sb("w_hi", [P, L], F32R)
        w_lo = sb("w_lo", [P, L], F32R)
        extra = [sb(f"extra{i}", [P, L], F32R) for i in range(4)]
        aT_sb = sb("aT_sb", [P, KC, ER])
        bfT_sb = sb("bfT_sb", [P, 2, L])
        bias_row = sb("bias_row", [1, L])
        er_w = sb("er_w", [P, 2])
        h_all = sb("h_all", [P, NSEQ * NT * E])

        idx_now = [sb(f"idx_now{p}", [P, NT], I32) for p in range(2)]
        gathered = [sb(f"gathered{p}", [P, NT, 2 * E]) for p in range(2)]
        et_hl = [sb(f"et_hl{p}", [P, SPAN], F32R) for p in range(2)]
        et_hh = [sb(f"et_hh{p}", [P, SPAN + 8], F32R) for p in range(2)]
        hT = [sb(f"hT{p}", [P, T]) for p in range(2)]
        u_hi = [sb(f"u_hi{p}", [P, T], F32R) for p in range(2)]
        u_lo = [sb(f"u_lo{p}", [P, T], F32R) for p in range(2)]
        xT = [sb(f"xT{p}", [P, 2 * P], F32R) for p in range(2)]
        a_sb = [sb(f"a_sb{p}", [P, NT]) for p in range(2)]
        mean_sb = [sb(f"mean_sb{p}", [P, NT]) for p in range(2)]
        u_row = sb("u_row", [P, NT, 2 * E + 1])
        odd = sb("odd", [P, T + 1])
        x_row = sb("x_row", [P, NT, XW], F32R)
        prod = sb("prod", [P, NT, E + 1])
        var = sb("var", [P, NT])
        lin = sb("lin", [P, NT])
        cert = sb("cert", [P, NT])
        cert_max = sb("cert_max", [P, NT])
        var_eps = sb("var_eps", [P, NT])
        inv_std = sb("inv_std", [P, NT])
        a_sq = sb("a_sq", [P, NT])
        var2 = sb("var2", [P, NT])
        var2_eps = sb("var2_eps", [P, NT])
        beta = sb("beta", [P, NT])
        inv_a = sb("inv_a", [P, NT])
        minus_half = sb("minus_half", [P, NT])
        obuf = sb("obuf", [P, 4, 2, L])
        verdict = sb("verdict", [P, 8])
        flag = sb("flag", [1, 1], I32)
        pad_col = sb("pad_col", [E, 1])
        xbar_col = sb("xbar_col", [P, KC])
        xbar_col_r = sb("xbar_col_r", [P, KC], F32R)
        g_ones = sb("g_ones", [1, P])
        g_row = sb("g_row", [P, 32])
        g_idx = sb("g_idx", [P, 8], U32)

        g_stats = sb("g_stats", [P, 12])
        g_mv = sb("g_mv", [P, 2])

        wT_sb = h_all[:, :].rearrange("p (c n) -> p c n", c=KC)
        wte_ld = odd[:, 1:1 + KC * E].rearrange("p (k e) -> p k e", k=KC)
        last_row = odd[0:1, 1 + KC * E:1 + KC * E + E]
        table_hl = u_hi[0][:, :].rearrange("p (k two e) -> p k two e", k=KC, two=2)
        last_hl = xT[1][0:1, 0:2 * E].rearrange("p (two e) -> p two e", two=2)
        w1_ld = obuf[:, 0, 0, :].rearrange("p (j n) -> p j n", j=J)
        w2cT = obuf[:, 0, 1, 0:KC * (E + 1)].rearrange("p (c n) -> p c n", c=KC)
        xa_sb = obuf[0:E + 1, 1, 0, 0:ER]
        xaT_sb = obuf[:, 1, 0, ER:ER + 2 * (E + 1)].rearrange("p (c n) -> p c n", c=2)
        g_hT = odd[:, 0:T]
        er_ld = obuf[:, 1, 0, 512:516]
        raw0 = obuf[:, 2, 0, 0:NT * E].rearrange("p (i e) -> p i e", i=NT)
        xbar_rows = xT[0][0:KC, 0:P]
        w2_hi, b_hi, b_lo = u_hi[1][0:E + 1, :], u_hi[1][E:E + 1, :], u_lo[1][E:E + 1, :]
        bias_hi, bias_lo = u_hi[1][0:1, :], u_lo[1][0:1, :]
        g_hi, g_lo = u_hi[1][96:97, :], u_lo[1][96:97, :]

        def hankel(c):
            return extra[c // 2][:, 512 * (c % 2):512 * (c % 2 + 1)]

        g_hT = odd[:, 0:T]
        er_ld = obuf[:, 1, 0, 512:516]

        o_ps = ps("o_ps", [P, 4, 512])
        conv_ps = ps("conv_ps", [P, 512])
        et_ps = ps("et_ps", [P, 512])
        sum_ps = ps("sum_ps", [P, 512])
        mix_ps = ps("mix_ps", [P, 512])

        def y_view(hh):
            return (mix_ps, sum_ps)[hh][:, 0:4 * (E + 3)].rearrange("p (i n) -> p i n", i=4)

        ids_in, table_in, w1_in, b1_in, consts_in, w2_in, small_in, aT_in, bfT_in, hankel_in = (
            sem(n) for n in ("ids_in", "table_in", "w1_in", "b1_in", "consts_in", "w2_in", "small_in", "aT_in", "bfT_in", "hankel_in"))
        wT_in = [sem(f"wT_in{n}") for n in range(KC // 2)]
        rows0_in = sem("rows0_in")
        rows0_split = sem("rows0_split")
        zeros_set = sem("zeros_set")
        table_hi_set = sem("table_hi_set")
        table_split = sem("table_split")
        table_stored = sem("table_stored")
        pads_hi = sem("pads_hi")
        pads_set = sem("pads_set")
        shift_hi_set = sem("shift_hi_set")
        shift_set = sem("shift_set")
        pad_conv_done = sem("pad_conv_done")
        pad_conv_kept = sem("pad_conv_kept")
        w2_sum = sem("w2_sum")
        w2_mean = sem("w2_mean")
        w2_centred = sem("w2_centred")
        w2T_done = sem("w2T_done")
        w2T_kept = sem("w2T_kept")
        ones_set = sem("ones_set")
        hbar_set = sem("hbar_set")
        mom_done = sem("mom_done")
        mom_kept = sem("mom_kept")
        xbar_stored = sem("xbar_stored")
        xa_done = sem("xa_done")
        xa_kept = sem("xa_kept")
        g_done = sem("g_done")
        w_hi_set = sem("w_hi_set")
        extra_zeroed = sem("extra_zeroed")
        w_set = sem("w_set")
        g_hi_set = sem("g_hi_set")
        row0_in, rows_in = sem("row0_in"), sem("rows_in")
        acf_done = sem("acf_done")
        acf_kept = sem("acf_kept")
        idx_ready = sem("idx_ready")
        rows_gathered = [sem(f"rows_gathered{p}") for p in range(2)]
        et_done = sem("et_done")
        et_kept = sem("et_kept")
        et_top_kept = sem("et_top_kept")
        et_back_kept = sem("et_back_kept")
        conv_done = sem("conv_done")
        odd_kept = sem("odd_kept")
        shifts_added = sem("shifts_added")
        tanh_done = sem("tanh_done")
        h_done = sem("h_done")
        h_ready = sem("h_ready")
        h_saved = sem("h_saved")
        y_done = sem("y_done")
        prod_ready = sem("prod_ready")
        var_ready = sem("var_ready")
        cert_step = sem("cert_step")
        scal_step = sem("scal_step")
        u_ready = sem("u_ready")
        x_step = sem("x_step")
        x_ready = sem("x_ready")
        ut_done = sem("ut_done")
        hi_kept = sem("hi_kept")
        lo_kept = sem("lo_kept")
        xt_done = sem("xt_done")
        xt_kept = sem("xt_kept")
        o_done = sem("o_done")
        oa_kept = sem("oa_kept")
        ov_kept = sem("ov_kept")
        stored = [sem(f"stored{q}") for q in range(4)]
        v_dve = sem("v_dve")
        v_pool = sem("v_pool")
        flag_set = sem("flag_set")
        g_pe, g_dve, g_act, g_pool = sem("g_pe"), sem("g_dve"), sem("g_act"), sem("g_pool")
        g_link = sem("g_link")
        pool_passed, sp_passed, dve_passed, pe_passed = (
            sem(f"{eng}_passed") for eng in ("pool", "sp", "dve", "pe"))
        g_table_in, g_stored = sem("g_table_in"), sem("g_stored")

        out_pairs = out.rearrange("s (q i p) o -> (s q) p i o", i=2, p=P)
        out_tiles = out.rearrange("s (i p) o -> (s i) p o", p=P)

        FIRST = 4

        def in_step(k, g, u):
            return isinstance(g, int) and 2 * g + u == k

        def steps(eng, step, after_step0, after_step1):
            for k in range(FIRST):
                step(k // 2, k % 2, True, k >= 1, k >= 2)
                if k == 0:
                    after_step0()
                if k == 1:
                    after_step1()
            with eng.Fori(FIRST // 2, NSEQ // 2) as g:
                step(g, 0, True, True, True)
                step(g, 1, True, True, True)
            for k in range(NSEQ, NSEQ + 2):
                step(k // 2, k % 2, False, k <= NSEQ, True)

        block = ctx.enter_context(nc.Block())

        @block.sync
        def _(sp):
            sp.dma_start(ids_sb[:, :], ids).then_inc(ids_in, 16)
            sp.dma_start(w2c[0:E, :], w2).then_inc(w2_in, 16)
            sp.dma_start(w2c[E:E + 1, :], b2).then_inc(w2_in, 16)
            sp.dma_start(ident_sb[:, :], ident).then_inc(consts_in, 16)
            sp.dma_start(b1_col[:, :], b1).then_inc(b1_in, 16)
            for half in range(2):
                sp.dma_start(w1_ld[E * half:E * half + E], w1.rearrange("(j e) n -> e j n", e=E)).then_inc(w1_in, 16)
            sp.dma_start(pad_col[:, :], wte[VOCAB:VOCAB + 1, :].rearrange("a e -> e a")).then_inc(table_in, 16)
            sp.dma_start(wte_ld, wte[0:VOCAB, :].rearrange("(p k) e -> p k e", k=KC)).then_inc(table_in, 16)
            sp.dma_start(last_row, wte[VOCAB:VOCAB + 1, :]).then_inc(table_in, 16)
            sp.dma_start(er_ld[:, 0:2], coeffs).then_inc(small_in, 16)
            sp.dma_start(er_ld[:, 2:4], scales).then_inc(small_in, 16)
            sp.dma_start(bias_row[:, :], bias).then_inc(small_in, 16)
            sp.wait_ge(table_split, 2)
            sp.dma_start(split_table[0:VOCAB, :].rearrange("(p k) e -> p k e", k=KC),
                         table_hl.bitcast(F32).rearrange("p k two e -> p k (two e)")).then_inc(table_stored, 16)
            sp.dma_start(split_table[VOCAB:VOCAB + 1, :],
                         last_hl.bitcast(F32).rearrange("p two e -> p (two e)")).then_inc(table_stored, 16)
            sp.dma_start(aT_sb[:, :, :], aT.rearrange("(c p) n -> p c n", p=P)).then_inc(aT_in, 16)
            for c in range(0, KC, 2):
                sp.dma_start(wT_sb[:, c:c + 2, :], wT[P * c:P * (c + 2), :].rearrange("(c p) n -> p c n", p=P)).then_inc(wT_in[c // 2], 16)
            sp.dma_start(bfT_sb[:, :, :], bfT.rearrange("(c p) n -> p c n", p=P)).then_inc(bfT_in, 16)
            sp.wait_ge(mom_kept, 5)
            for n in range(2):
                sp.dma_start(xbar_twice[L * n:L * (n + 1)].rearrange("(c p) -> c p", p=P), xbar_rows.bitcast(F32)).then_inc(xbar_stored, 16)
            sp.wait_ge(xbar_stored, 32)
            for c in range(KC):
                sp.dma_start(hankel(c).bitcast(F32), bass.AP(xbar_twice.tensor, P * c + 1, [[1, P], [1, 512]])).then_inc(hankel_in, 16)
            sp.wait_ge(extra_zeroed, 1)
            sp.wait_ge(w_set, 3)
            for n, row in ((0, b_hi), (1, b_lo), (5, bias_hi), (6, bias_lo), (7, bias_hi)):
                sp.dma_start(extra[0][n:n + 1, :].bitcast(F32), row.bitcast(F32)).then_inc(row0_in, 16)
            sp.wait_ge(w_set, 4)
            for n, row in ((2, g_hi), (3, g_lo), (4, g_hi)):
                sp.dma_start(extra[0][n:n + 1, :].bitcast(F32), row.bitcast(F32)).then_inc(row0_in, 16)
            sp.wait_ge(row0_in, 16 * NX)
            for i in range(1, 4):
                sp.dma_start(extra[i][XW * i:XW * i + NX, :].bitcast(F32), extra[0][0:NX, :].bitcast(F32)).then_inc(rows_in, 16)

            def step(g, u, front, mid, back):
                if back:
                    c = 2 * (g - 1) + u
                    for q in range(4):
                        sp.wait_ge(oa_kept, NT * c + 2 * q + 2)
                        sp.wait_ge(ov_kept, NT * c + 2 * q + 2)
                        sp.dma_start(out_pairs[bass.ds(4 * c + q, 1)].rearrange("a p i o -> (a p) i o"),
                                     obuf[:, q, :, :]).then_inc(stored[q], 16)

            steps(sp, step, lambda: None, lambda: None)
            for q in range(4):
                sp.wait_ge(stored[q], 16 * NSEQ)
            sp.wait_ge(table_stored, 32)

            sp.wait_ge(flag_set, 1)
            need = sp.value_load(flag[0:1, 0:1], min_val=0, max_val=1)
            table = obuf[:, :, :, :].rearrange("p a b n -> p (a b) n")
            with sp.If(need != 0):
                with sp.Fori(0, NSEQ * NT) as t:
                    for n, (src, used, count) in enumerate((
                            (dft, g_dve, 10 * t + 1), (acf, g_pe, 11 * t + 4), (lags, g_pe, 11 * t + 5),
                            (dft, g_dve, 10 * t + 5), (idft, g_pe, 11 * t + 7), (wT, g_pe, 11 * t + 8))):
                        sp.wait_ge(used, count)
                        dst, rows = (table[:, 0, :], src) if n == 2 else (table, src.rearrange("(c p) n -> p c n", p=P))
                        sp.dma_start(dst, rows).then_inc(g_table_in, 16)
                        wait_alone(sp, g_table_in, 96 * t + 16 * n + 16, sp_passed)
                    sp.wait_ge(g_dve, 10 * t + 10)
                    sp.dma_start(out_tiles[bass.ds(t, 1)].rearrange("a p o -> (a p) o"), g_hT[:, :]).then_inc(g_stored, 16)
                    wait_alone(sp, g_stored, 16 * t + 16, sp_passed)

        @block.gpsimd
        def _(pool):
            def gather(s, p, uses):
                ge(pool, et_done, uses)
                pool.tensor_copy(idx_now[p][:, :], ids_sb[:, bass.ds(NT * s, NT)]).then_inc(idx_ready, 1)
                wait_alone(pool, idx_ready, s + 1, pool_passed)

            def gather_rows(p, i):
                pool.indirect_dma_start(
                    gathered[p][:, i, :], None, split_table,
                    bass.IndirectOffsetOnAxis(ap=idx_now[p][:, i:i + 1].bitcast(U32), axis=0),
                ).then_inc(rows_gathered[p], 16)

            pool.wait_ge(ids_in, 16)
            gather(0, 0, 0)
            for i in range(NT):
                pool.indirect_dma_start(
                    raw0[:, i, :], None, wte,
                    bass.IndirectOffsetOnAxis(ap=idx_now[0][:, i:i + 1].bitcast(U32), axis=0),
                ).then_inc(rows0_in, 16)
            pool.memset(x_row[:, :, :].bitcast(F32), 0.0)
            pool.memset(minus_half[:, :], -0.5)
            pool.memset(g_ones[:, :], 1.0)
            pool.memset(cert_max[:, :], -3.0e38)
            pool.memset(u_row[:, :, 2 * E:2 * E + 1], 1.0).then_inc(zeros_set, 1)
            pool.wait_ge(zeros_set, 1)
            pool.memset(x_row[:, :, 0:2].bitcast(F32), 1.0).then_inc(zeros_set, 1)
            pool.wait_ge(table_stored, 32)

            def step(g, u, front, mid, back, last=False):
                a, b = 2 * g + u, 2 * g + u - 1
                more = front and not last
                if more:
                    gather(a + 1, 1 - u, 2 * a)
                    for i in range(NT // 2):
                        gather_rows(1 - u, i)
                if in_step(1, g, u):
                    pool.wait_ge(acf_done, 1)
                    for i in range(4):
                        last_fill = pool.memset(extra[i][:, :].bitcast(F32), 0.0)
                    last_fill.then_inc(extra_zeroed, 1)
                if mid:
                    pb = 1 - u
                    wait_alone(pool, var_ready, 2 * b + 2, pool_passed)
                    pool.tensor_scalar(var_eps[:, :], var[:, :], EPS, None, ALU.add).then_inc(scal_step, 1)
                    wait_alone(pool, scal_step, 7 * b + 1, pool_passed)
                    pool.tensor_tensor(inv_std[:, :], var_eps[:, :], minus_half[:, :], ALU.pow).then_inc(scal_step, 1)
                    wait_alone(pool, scal_step, 7 * b + 2, pool_passed)
                    pool.tensor_scalar(a_sb[pb][:, :], inv_std[:, :], 1.0, None, ALU.add).then_inc(scal_step, 1)
                    wait_alone(pool, scal_step, 7 * b + 3, pool_passed)
                    pool.tensor_tensor(a_sq[:, :], a_sb[pb][:, :], a_sb[pb][:, :], ALU.mult).then_inc(scal_step, 1)
                    wait_alone(pool, scal_step, 7 * b + 4, pool_passed)
                    pool.tensor_tensor(var2[:, :], a_sq[:, :], var[:, :], ALU.mult).then_inc(scal_step, 1)
                    wait_alone(pool, scal_step, 7 * b + 5, pool_passed)
                    pool.tensor_scalar(var2_eps[:, :], var2[:, :], EPS, None, ALU.add).then_inc(scal_step, 1)
                    wait_alone(pool, scal_step, 7 * b + 6, pool_passed)
                    pool.tensor_tensor(beta[:, :], var2_eps[:, :], minus_half[:, :], ALU.pow).then_inc(scal_step, 1)
                    if in_step(1, g, u):
                        pool.wait_ge(g_done, 1)
                    pool.wait_ge(h_ready, b + 1)
                    pool.tensor_copy(h_all[:, bass.ds(NT * E * b, NT * E)].rearrange("p (i e) -> p i e", i=NT),
                                     u_row[:, :, E:2 * E]).then_inc(h_saved, 1)
                if more:
                    for i in range(NT // 2, NT):
                        gather_rows(1 - u, i)

            for k in range(FIRST):
                step(k // 2, k % 2, True, k >= 1, k >= 2)
            with pool.Fori(FIRST // 2, NSEQ // 2 - 1) as g:
                step(g, 0, True, True, True)
                step(g, 1, True, True, True)
            for k in range(NSEQ - 2, NSEQ + 2):
                step(k // 2, k % 2, k < NSEQ, k <= NSEQ, True, last=k == NSEQ - 1)

            pool.wait_ge(v_dve, 1)
            pool.partition_all_reduce(verdict[:, 4:5], verdict[:, 3:4], P, bass.bass_isa.ReduceOp.max).then_inc(v_pool, 1)

            pool.wait_ge(flag_set, 1)
            need = pool.value_load(flag[0:1, 0:1], min_val=0, max_val=1)
            with pool.If(need != 0):
                with pool.Fori(0, NSEQ * NT) as t:
                    for n in range(2):
                        pool.wait_ge(g_dve, 10 * t + (2, 7)[n])
                        pool.tensor_tensor(g_row[:, 4 * n + 1:4 * n + 2], g_row[:, 4 * n:4 * n + 1],
                                           minus_half[:, 0:1], ALU.pow).then_inc(g_pool, 1)

        @block.scalar
        def _(act):
            act.wait_ge(b1_in, 16)
            nc.scalar.activation(hbar[0:E, :], b1_col[:, 0:1].to_broadcast([E, P]), ACT.Tanh).then_inc(hbar_set, 1)
            act.wait_ge(w2T_done, 1)
            for n, bank in enumerate((sum_ps, mix_ps)):
                nc.scalar.copy(w2cT[:, 4 * n:4 * n + 4, :],
                               bank[:, 0:4 * (E + 1)].rearrange("p (c n) -> p c n", c=4)).then_inc(w2T_kept, 1)

            act.wait_ge(w1_in, 32)
            nc.scalar.copy(shift_hi[:, :, :], w1_ld).then_inc(shift_hi_set, 1)
            act.wait_ge(pad_conv_done, 1)
            act.wait_ge(table_split, 2)
            nc.scalar.copy(odd[0:E, 0:1], conv_ps[E:P, 0:1]).then_inc(pad_conv_kept, 1)

            def tile_out(c, pc, i):
                q = i // 2
                if i % 2 == 0:
                    ge(act, stored[q], 16 * c)
                act.wait_ge(o_done, NT * c + i + 1)
                nc.scalar.activation(obuf[:, q, i % 2, 0:512], o_ps[:, 2 * (i % 2), :], ACT.Identity,
                                     bias=mean_sb[pc][:, i:i + 1], scale=a_sb[pc][:, i:i + 1]).then_inc(oa_kept, 1)

            def step(g, u, front, mid, back):
                a, b, c = 2 * g + u, 2 * g + u - 1, 2 * (g - 1) + u
                pb = 1 - u

                def keep_et(hh):
                    act.wait_ge(et_done, 2 * a + hh + 1)
                    col = PAD + HALF * hh
                    nc.scalar.copy(et_hl[u][:, col:col + HALF], et_ps[:, :]).then_inc(et_kept, 1)
                    nc.scalar.copy(et_hh[u][E:P, col + 8:col + 8 + HALF], et_ps[0:E, :]).then_inc(et_back_kept, 1)

                def keep_odd(hh):
                    act.wait_ge(conv_done, 2 * a + hh + 1)
                    ge(act, shifts_added, 2 * a + hh)
                    n = HALF - hh
                    nc.scalar.copy(odd[0:E, HALF * hh + 1:HALF * hh + 1 + n], conv_ps[E:P, 0:n]).then_inc(odd_kept, 1)

                def take_tanh(hh):
                    act.wait_ge(shifts_added, 2 * a + hh + 1)
                    cols = slice(HALF * hh, HALF * (hh + 1))
                    nc.scalar.activation(hT[u][0:E, cols], hT[u][0:E, cols], ACT.Tanh,
                                         bias=b1_col[:, 0:1]).then_inc(tanh_done, 1)

                if back:
                    tile_out(c, u, 0)
                if mid:
                    act.wait_ge(h_done, b + 1)
                    ge(act, h_saved, b)
                    nc.scalar.copy(u_row[:, :, E:2 * E],
                                   sum_ps[:, :].rearrange("p (i e) -> p i e", i=NT)).then_inc(h_ready, 1)
                if front:
                    keep_et(0)
                if back:
                    tile_out(c, u, 1)
                if front:
                    keep_et(1)
                if back:
                    tile_out(c, u, 2)
                    tile_out(c, u, 3)
                if in_step(1, g, u):
                    act.wait_ge(g_done, 1)
                    nc.scalar.copy(g_hi, o_ps[E:E + 1, 0:2, :].rearrange("p a n -> p (a n)")).then_inc(g_hi_set, 1)
                if front:
                    keep_odd(0)
                if back:
                    tile_out(c, u, 4)
                if front:
                    take_tanh(0)
                if back:
                    tile_out(c, u, 5)
                if mid:
                    for hh, bank in enumerate((sum_ps, mix_ps)):
                        act.wait_ge(ut_done, 2 * b + hh + 1)
                        nc.scalar.copy(u_hi[pb][:, HALF * hh:HALF * (hh + 1)], bank[:, :]).then_inc(hi_kept, 1)
                    act.wait_ge(xt_done, b + 1)
                    nc.scalar.copy(xT[pb][:, :], et_ps[:, 0:2 * P]).then_inc(xt_kept, 1)
                if front:
                    keep_odd(1)
                if front:
                    take_tanh(1)
                if back:
                    tile_out(c, u, 6)
                    tile_out(c, u, 7)

            steps(act, step, lambda: None, lambda: None)

            act.wait_ge(flag_set, 1)
            need = act.value_load(flag[0:1, 0:1], min_val=0, max_val=1)
            with act.If(need != 0):
                with act.Fori(0, NSEQ * NT) as t:
                    act.wait_ge(g_pe, 11 * t + 1)
                    nc.scalar.copy(g_hT[0:E + 1, 0:P], mix_ps[0:E + 1, 0:P]).then_inc(g_act, 1)
                    act.wait_ge(g_pe, 11 * t + 3)
                    nc.scalar.copy(hT[1][:, :], o_ps[:, 2:4, :].rearrange("p a n -> p (a n)")).then_inc(g_act, 1)
                    act.wait_ge(g_pe, 11 * t + 4)
                    spec = gathered[0][:, :, :].rearrange("p i n -> p (i n)")
                    nc.scalar.copy(spec, o_ps[:, 0:2, :].rearrange("p a n -> p (a n)"))
                    nc.scalar.activation(gathered[1][:, :, :].rearrange("p i n -> p (i n)"),
                                         o_ps[:, 0:2, :].rearrange("p a n -> p (a n)"), ACT.Square).then_inc(g_act, 1)
                    act.wait_ge(g_dve, 10 * t + 4)
                    nc.scalar.activation(g_row[:, 16:16 + TOPK], g_row[:, 8:8 + TOPK], ACT.Exp, bias=g_row[:, 3:4],
                                         accum_out=g_row[:, 2:3]).then_inc(g_act, 1)
                    act.wait_ge(g_pe, 11 * t + 6)
                    nc.scalar.copy(hT[1][:, :], o_ps[:, 2:4, :].rearrange("p a n -> p (a n)")).then_inc(g_act, 1)
                    act.wait_ge(g_pe, 11 * t + 7)
                    nc.scalar.copy(gathered[1][:, :, :].rearrange("p i n -> p (i n)"),
                                   o_ps[:, 0:2, :].rearrange("p a n -> p (a n)")).then_inc(g_act, 1)
                    act.wait_ge(g_pe, 11 * t + 9)
                    nc.scalar.copy(hT[1][:, :], o_ps[:, 2:4, :].rearrange("p a n -> p (a n)")).then_inc(g_act, 1)

        @block.vector
        def _(dve):
            for tile in (hbar, hT[0], hT[1]):
                nc.vector.memset(tile[E:E + 1, :], 1.0).then_inc(ones_set, 1)
            dve.wait_ge(w2_in, 32)
            nc.vector.reduce_sum(w2mean[:, :], w2c[:, :], AX.X).then_inc(w2_sum, 1)
            dve.wait_ge(w2_sum, 1)
            nc.vector.tensor_scalar(w2mean[:, :], w2mean[:, :], 1.0 / L, None, ALU.mult).then_inc(w2_mean, 1)
            dve.wait_ge(w2_mean, 1)
            nc.vector.tensor_scalar(w2c[:, :], w2c[:, :], w2mean[:, 0:1], None, ALU.subtract).then_inc(w2_centred, 1)
            dve.wait_ge(table_in, 48)
            nc.vector.tensor_copy(table_hl[:, :, 0, :], wte_ld)
            nc.vector.tensor_copy(last_hl[:, 0, :], last_row)
            for p in range(2):
                nc.vector.tensor_copy(et_hl[p][0:E, 0:PAD], pad_col[:, 0:1].to_broadcast([E, PAD]))
                nc.vector.tensor_copy(et_hh[p][0:E, 0:PAD], pad_col[:, 0:1].to_broadcast([E, PAD]))
                last = nc.vector.tensor_copy(et_hh[p][E:P, 0:PAD + 8], pad_col[:, 0:1].to_broadcast([E, PAD + 8]))
            last.then_inc(table_hi_set, 1)
            dve.wait_ge(table_hi_set, 1)
            nc.vector.tensor_tensor(table_hl[:, :, 1, :], wte_ld, table_hl[:, :, 0, :].bitcast(F32),
                                    ALU.subtract).then_inc(table_split, 1)
            nc.vector.tensor_tensor(last_hl[:, 1, :], last_row, last_hl[:, 0, :].bitcast(F32),
                                    ALU.subtract).then_inc(table_split, 1)
            for p in range(2):
                nc.vector.tensor_tensor(et_hl[p][E:P, 0:PAD], pad_col[:, 0:1].to_broadcast([E, PAD]),
                                        et_hl[p][0:E, 0:PAD].bitcast(F32), ALU.subtract).then_inc(pads_set, 1)
            dve.wait_ge(shift_hi_set, 1)
            for half in range(2):
                rows, js = slice(E * half, E * half + E), slice(J // 2 * half, J // 2 * (half + 1))
                nc.vector.tensor_tensor(shift_lo[rows, :, :], w1_ld[rows, js, :], shift_hi[rows, js, :].bitcast(F32),
                                        ALU.subtract).then_inc(shift_set, 1)
            dve.wait_ge(mom_done, 1)
            nc.vector.tensor_copy(moments[:, E + 1:E + 2], w2mean[:, :])
            nc.vector.tensor_scalar(moments[:, 0:E + 1], o_ps[0:E + 1, 0, 0:E + 1], 1.0 / L, None,
                                    ALU.mult).then_inc(mom_kept, 1)
            dve.wait_ge(mom_done, 2)
            nc.vector.tensor_copy(moments[:, E + 2:E + 3], o_ps[0:E + 1, 1, 0:1]).then_inc(mom_kept, 1)
            dve.wait_ge(mom_done, 3)
            nc.vector.tensor_copy(verdict[:, 0:1], o_ps[:, 2, 0:1]).then_inc(mom_kept, 1)
            dve.wait_ge(rows0_in, 16 * NT)
            nc.vector.tensor_copy(gathered[0][:, :, 0:E].bitcast(F32R), raw0).then_inc(rows0_split, 1)
            dve.wait_ge(rows0_split, 1)
            nc.vector.tensor_tensor(gathered[0][:, :, E:2 * E].bitcast(F32R), raw0, gathered[0][:, :, 0:E],
                                    ALU.subtract).then_inc(rows0_split, 1)
            dve.wait_ge(mom_done, 4)
            nc.vector.tensor_copy(xbar_col_r[:, :], o_ps[:, 3, 0:KC])
            nc.vector.tensor_copy(xbar_col[:, :], o_ps[:, 3, 0:KC]).then_inc(mom_kept, 1)
            dve.wait_ge(mom_done, 5)
            nc.vector.tensor_copy(xbar_rows, o_ps[0:KC, 0, 0:P]).then_inc(mom_kept, 1)
            def tile_out(c, pc, i):
                q = i // 2
                if i % 2 == 0:
                    ge(dve, stored[q], 16 * c)
                dve.wait_ge(o_done, NT * c + i + 1)
                nc.vector.tensor_scalar(obuf[:, q, i % 2, 512:L], o_ps[:, 2 * (i % 2) + 1, :], a_sb[pc][:, i:i + 1],
                                        mean_sb[pc][:, i:i + 1], ALU.mult, ALU.add).then_inc(ov_kept, 1)

            def keep_xa():
                dve.wait_ge(small_in, 48)
                nc.vector.tensor_tensor(er_w[:, :], er_ld[:, 0:2], er_ld[:, 2:4], ALU.mult).then_inc(xa_kept, 1)
                dve.wait_ge(xa_done, 1)
                nc.vector.tensor_copy(xa_sb, sum_ps[0:E + 1, 0:ER]).then_inc(xa_kept, 1)

            def weight_halves():
                nc.vector.tensor_copy(w_hi[E:P, :], w2c[0:E, :])
                nc.vector.tensor_copy(w2_hi, w2c[:, :]).then_inc(w_hi_set, 1)
                dve.wait_ge(w_hi_set, 1)
                nc.vector.tensor_tensor(w_lo[E:P, :], w2c[0:E, :], w2_hi[0:E, :].bitcast(F32), ALU.subtract).then_inc(w_set, 1)
                nc.vector.tensor_tensor(b_lo, w2c[E:E + 1, :], b_hi.bitcast(F32), ALU.subtract).then_inc(w_set, 1)
                dve.wait_ge(w_set, 1)
                nc.vector.tensor_copy(bias_hi, bias_row[:, :]).then_inc(w_hi_set, 1)
                dve.wait_ge(w_hi_set, 2)
                nc.vector.tensor_tensor(bias_lo, bias_row[:, :], bias_hi.bitcast(F32), ALU.subtract).then_inc(w_set, 1)

            def g_halves():
                dve.wait_ge(g_done, 1)
                gw = o_ps[0:E, 0:2, :].rearrange("p a n -> p (a n)")
                gb = o_ps[E:E + 1, 0:2, :].rearrange("p a n -> p (a n)")
                nc.vector.tensor_copy(w_hi[0:E, :], gw).then_inc(w_hi_set, 1)
                dve.wait_ge(g_hi_set, 1)
                nc.vector.tensor_tensor(g_lo, gb, g_hi.bitcast(F32), ALU.subtract).then_inc(w_set, 1)
                dve.wait_ge(w_hi_set, 3)
                nc.vector.tensor_tensor(w_lo[0:E, :], gw, w_hi[0:E, :].bitcast(F32), ALU.subtract).then_inc(w_set, 1)

            def step(g, u, front, mid, back):
                a, b, c = 2 * g + u, 2 * g + u - 1, 2 * (g - 1) + u
                pb = 1 - u

                def keep_et_top(hh):
                    dve.wait_ge(et_kept, 2 * a + hh + 1)
                    col = PAD + HALF * hh
                    nc.vector.tensor_copy(et_hh[u][0:E, col:col + HALF],
                                          et_hl[u][0:E, col:col + HALF].bitcast(F32)).then_inc(et_top_kept, 1)

                def add_shifts(hh):
                    dve.wait_ge(odd_kept, 2 * a + hh + 1)
                    cols = slice(HALF * hh, HALF * (hh + 1))
                    nc.vector.tensor_tensor(hT[u][0:E, cols], conv_ps[0:E, :], odd[0:E, cols], ALU.add).then_inc(shifts_added, 1)

                def variance(hh):
                    tiles = slice(4 * hh, 4 * hh + 4)
                    dve.wait_ge(h_ready, b + 1)
                    dve.wait_ge(y_done, 2 * b + hh + 1)
                    y = y_view(hh)
                    nc.vector.tensor_tensor(prod[:, tiles, :], y[:, :, 0:E + 1], u_row[:, tiles, E:2 * E + 1],
                                            ALU.mult).then_inc(prod_ready, 1)
                    nc.vector.tensor_copy(mean_sb[pb][:, tiles], y[:, :, E + 1])
                    nc.vector.tensor_copy(lin[:, tiles], y[:, :, E + 2])
                    dve.wait_ge(prod_ready, 2 * b + hh + 1)
                    nc.vector.tensor_reduce(var[:, tiles], prod[:, tiles, :], AX.X, ALU.add).then_inc(var_ready, 1)

                def scale_h():
                    dve.wait_ge(scal_step, 7 * b + 7)
                    nc.vector.tensor_tensor(u_row[:, :, 0:E], u_row[:, :, E:2 * E],
                                            beta[:, :].unsqueeze(2).to_broadcast([P, NT, E]), ALU.mult).then_inc(u_ready, 1)
                    nc.vector.reciprocal(inv_a[:, :], a_sb[pb][:, :]).then_inc(x_step, 1)
                    nc.vector.tensor_copy(x_row[:, :, 2:4], beta[:, :].unsqueeze(2).to_broadcast([P, NT, 2])).then_inc(x_step, 1)
                    dve.wait_ge(x_step, 3 * b + 1)
                    nc.vector.tensor_copy(x_row[:, :, 5:7], inv_a[:, :].unsqueeze(2).to_broadcast([P, NT, 2])).then_inc(x_step, 1)
                    dve.wait_ge(x_step, 3 * b + 2)
                    nc.vector.tensor_tensor(x_row[:, :, 4], beta[:, :], x_row[:, :, 2].bitcast(F32), ALU.subtract)
                    dve.wait_ge(x_step, 3 * b + 3)
                    nc.vector.tensor_tensor(x_row[:, :, 7], inv_a[:, :], x_row[:, :, 5].bitcast(F32),
                                            ALU.subtract).then_inc(x_ready, 1)

                if back:
                    tile_out(c, u, 0)
                if front:
                    keep_et_top(0)
                if back:
                    tile_out(c, u, 1)
                if front:
                    keep_et_top(1)
                if mid:
                    variance(0)
                if back:
                    tile_out(c, u, 2)
                if mid:
                    variance(1)
                if back:
                    tile_out(c, u, 3)
                if mid:
                    dve.wait_ge(var_ready, 2 * b + 2)
                    nc.vector.tensor_scalar(cert[:, :], var[:, :], 2 * GAP + 4 * L, None, ALU.mult).then_inc(cert_step, 1)
                    dve.wait_ge(cert_step, 3 * b + 1)
                    nc.vector.scalar_tensor_tensor(cert[:, :], lin[:, :], -8.0 * L, cert[:, :], ALU.mult,
                                                   ALU.add).then_inc(cert_step, 1)
                    dve.wait_ge(cert_step, 3 * b + 2)
                    nc.vector.tensor_tensor(cert_max[:, :], cert_max[:, :], cert[:, :], ALU.max).then_inc(cert_step, 1)
                if in_step(1, g, u):
                    weight_halves()
                    scale_h()
                    g_halves()
                if front:
                    add_shifts(0)
                if back:
                    tile_out(c, u, 4)
                if mid and not in_step(1, g, u):
                    scale_h()
                if back:
                    tile_out(c, u, 5)
                if mid:
                    for hh, bank in enumerate((sum_ps, mix_ps)):
                        dve.wait_ge(hi_kept, 2 * b + hh + 1)
                        cols = slice(HALF * hh, HALF * (hh + 1))
                        nc.vector.tensor_tensor(u_lo[pb][:, cols], bank[:, :], u_hi[pb][:, cols].bitcast(F32),
                                                ALU.subtract).then_inc(lo_kept, 1)
                if in_step(0, g, u):
                    keep_xa()
                if front:
                    add_shifts(1)
                if back:
                    tile_out(c, u, 6)
                    tile_out(c, u, 7)

            def after_step0():
                dve.wait_ge(xa_kept, 1)
                dve.wait_ge(xa_done, 2)
                for n in range(2):
                    nc.vector.tensor_scalar(xaT_sb[:, n, :], mix_ps[:, (E + 1) * n:(E + 1) * (n + 1)], er_w[:, n:n + 1],
                                            None, ALU.mult).then_inc(xa_kept, 1)

            def after_step1():
                dve.wait_ge(acf_done, 1)
                nc.vector.reduce_max(verdict[0:1, 1:2], o_ps[0:1, 2, :], AX.X).then_inc(acf_kept, 1)
                dve.wait_ge(acf_kept, 1)
                nc.vector.scalar_tensor_tensor(verdict[0:1, 2:3], o_ps[0:1, 3, 0:1], 1.0 - 1.0 / 512, verdict[0:1, 1:2],
                                               ALU.mult, ALU.subtract).then_inc(acf_kept, 1)

            steps(dve, step, after_step0, after_step1)

            dve.wait_ge(cert_step, 3 * NSEQ)
            nc.vector.reduce_max(verdict[:, 3:4], cert_max[:, :], AX.X).then_inc(v_dve, 1)
            dve.wait_ge(v_pool, 1)
            nc.vector.scalar_tensor_tensor(verdict[0:1, 5:6], verdict[0:1, 0:1], 4.0 * L, verdict[0:1, 4:5], ALU.mult,
                                           ALU.add).then_inc(v_dve, 1)
            dve.wait_ge(v_dve, 2)
            nc.vector.tensor_scalar(verdict[0:1, 6:7], verdict[0:1, 2:3], 0.98, -2 * GAP * EPS, ALU.mult,
                                    ALU.add).then_inc(v_dve, 1)
            dve.wait_ge(v_dve, 3)
            nc.vector.tensor_tensor(verdict[0:1, 7:8], verdict[0:1, 5:6], verdict[0:1, 6:7], ALU.is_le).then_inc(v_dve, 1)
            dve.wait_ge(v_dve, 4)
            scale, shift = (0.0, 1.0) if force_general else (-1.0, 1.0)
            nc.vector.tensor_scalar(flag[:, :], verdict[0:1, 7:8], scale, shift, ALU.mult, ALU.add).then_inc(flag_set, 1)

            dve.wait_ge(flag_set, 1)
            need = dve.value_load(flag[0:1, 0:1], min_val=0, max_val=1)
            with dve.If(need != 0):
                ab0, ab1 = hT[0][:, :], hT[1][:, :]
                rows = u_row[:, :, :].rearrange("p i n -> p (i n)")[:, 0:L]
                spec_x, spec_w = (gathered[n][:, :, :].rearrange("p i n -> p (i n)") for n in range(2))
                left, right = (o_ps[:, n:n + 2, :].rearrange("p a n -> p (a n)") for n in (0, 2))
                lag_row = obuf[:, 0, 0, :]
                LINKS = 26
                with dve.Fori(0, NSEQ * NT) as t:
                    count = [0]

                    def link(ins):
                        count[0] += 1
                        ins.then_inc(g_link, 1)
                        wait_alone(dve, g_link, LINKS * t + count[0], dve_passed)

                    def variance_eps(src, col):
                        for n in range(2):
                            last = nc.vector.bn_stats(g_stats[:, 6 * n:6 * n + 6], src[:, 512 * n:512 * (n + 1)])
                        link(last)
                        link(nc.vector.bn_aggr(g_mv[:, :], g_stats[:, :]))
                        nc.vector.tensor_scalar(g_row[:, col:col + 1], g_mv[:, 1:2], EPS, None, ALU.add).then_inc(g_dve, 1)

                    link(nc.vector.tensor_copy(prod[:, 0, 0:E], h_all[:, bass.ds(E * t, E)]))
                    nc.vector.memset(prod[:, 0, E:E + 1], 1.0).then_inc(g_dve, 1)
                    dve.wait_ge(g_pe, 11 * t + 2)
                    variance_eps(left, 0)
                    link(nc.vector.tensor_copy(g_row[:, 6:7], sum_ps[:, 0:1]))
                    link(nc.vector.tensor_scalar(rows, left, g_row[:, 6:7], None, ALU.add))
                    dve.wait_ge(g_pool, 2 * t + 1)
                    nc.vector.tensor_scalar(ab0, left, g_mv[:, 0:1], g_row[:, 1:2], ALU.subtract, ALU.mult).then_inc(g_dve, 1)
                    dve.wait_ge(g_pe, 11 * t + 5)
                    link(nc.vector.tensor_copy(ab0, right))
                    link(nc.vector.max(g_row[:, 8:16], ab0))
                    link(nc.vector.max_index(g_idx[:, :], g_row[:, 8:16], ab0))
                    nc.vector.tensor_copy(g_row[:, 24:32], g_idx[:, :])
                    link(nc.vector.tensor_scalar(g_row[:, 3:4], g_row[:, 8:9], -1.0, None, ALU.mult))
                    nc.vector.tensor_scalar(g_row[:, 7:8], g_row[:, 8:9], -1.0, None, ALU.mult).then_inc(g_dve, 1)
                    dve.wait_ge(g_act, 7 * t + 4)
                    link(nc.vector.reciprocal(g_row[:, 2:3], g_row[:, 2:3]))
                    link(nc.vector.tensor_scalar(g_row[:, 16:16 + TOPK], g_row[:, 16:16 + TOPK], g_row[:, 2:3], None, ALU.mult))
                    dve.wait_ge(g_table_in, 96 * t + 48)
                    link(nc.vector.tensor_scalar(ab0, lag_row, g_row[:, 24:25], g_row[:, 16:17], ALU.is_equal, ALU.mult))
                    for n in range(1, TOPK):
                        link(nc.vector.tensor_scalar(left, lag_row, g_row[:, 24 + n:25 + n], g_row[:, 16 + n:17 + n],
                                                     ALU.is_equal, ALU.mult))
                        add = nc.vector.tensor_tensor(ab0, ab0, left, ALU.add)
                        if n < TOPK - 1:
                            link(add)
                    add.then_inc(g_dve, 1)
                    dve.wait_ge(g_act, 7 * t + 6)
                    h_ = L // 2
                    xc, xs, wc, ws = spec_x[:, 0:h_], spec_x[:, h_:L], spec_w[:, 0:h_], spec_w[:, h_:L]
                    nc.vector.tensor_tensor(ab0[:, 0:h_], xc, wc, ALU.mult)
                    nc.vector.tensor_tensor(ab0[:, h_:L], xs, wc, ALU.mult)
                    nc.vector.tensor_tensor(left[:, 0:h_], xs, ws, ALU.mult)
                    link(nc.vector.tensor_tensor(left[:, h_:L], xc, ws, ALU.mult))
                    nc.vector.tensor_tensor(ab0[:, 0:h_], ab0[:, 0:h_], left[:, 0:h_], ALU.add)
                    link(nc.vector.tensor_tensor(ab0[:, h_:L], ab0[:, h_:L], left[:, h_:L], ALU.subtract))
                    nc.vector.tensor_tensor(ab0[0:1, 0:P], xc[0:1, 0:P], wc[0:1, 0:P], ALU.mult)
                    nc.vector.tensor_tensor(ab0[0:1, h_:h_ + P], xs[0:1, 0:P], ws[0:1, 0:P], ALU.mult).then_inc(g_dve, 1)
                    dve.wait_ge(g_pe, 11 * t + 8)
                    link(nc.vector.tensor_tensor(rows, rows, left, ALU.add))
                    variance_eps(rows, 4)
                    dve.wait_ge(g_pool, 2 * t + 2)
                    nc.vector.tensor_scalar(ab0, rows, g_mv[:, 0:1], g_row[:, 5:6], ALU.subtract, ALU.mult).then_inc(g_dve, 1)
                    dve.wait_ge(g_pe, 11 * t + 10)
                    for n in range(2):
                        last = nc.vector.tensor_scalar(spec_w[:, P * n:P * (n + 1)], sum_ps[:, P * n:P * (n + 1)],
                                                       er_w[:, n:n + 1], None, ALU.mult)
                    last.then_inc(g_dve, 1)
                    dve.wait_ge(g_pe, 11 * t + 11)
                    nc.vector.tensor_tensor(g_hT[:, :], rows, left, ALU.add).then_inc(g_dve, 1)
                    dve.wait_ge(g_stored, 16 * t + 16)
                    assert count[0] == LINKS, count


        @block.tensor
        def _(pe):
            mm, tr = nc.tensor.matmul, nc.tensor.transpose

            pe.wait_ge(consts_in, 16)
            pe.wait_ge(w2_centred, 1)
            for c in range(KC):
                bank = (sum_ps, mix_ps)[c // 4]
                last = tr(bank[:, (E + 1) * (c % 4):(E + 1) * (c % 4 + 1)], w2c[:, P * c:P * (c + 1)], ident_sb[0:E + 1, 0:E + 1])
            last.then_inc(w2T_done, 1)
            pe.wait_ge(w2T_kept, 2)
            for c in range(KC):
                last = mm(o_ps[0:E + 1, 0, 0:E + 1], w2cT[:, c, :], w2cT[:, c, :], start=(c == 0), stop=(c == KC - 1))
            last.then_inc(mom_done, 1)
            pe.wait_ge(mom_kept, 1)
            pe.wait_ge(hbar_set, 1)
            pe.wait_ge(ones_set, 1)
            mm(o_ps[0:E + 1, 1, 0:1], moments[:, 0:E + 1], hbar[:, 0:1], start=True, stop=True).then_inc(mom_done, 1)
            pe.wait_ge(mom_kept, 2)
            mm(o_ps[:, 2, 0:1], hbar[:, :], moments[:, E + 2:E + 3], start=True, stop=True).then_inc(mom_done, 1)

            def conv(u, col, width):
                for m in range(J // 2):
                    mm(conv_ps[:, 0:width], shift_hi[:, 2 * m:2 * m + 2, :], et_hl[u][:, col - 2 * m:col - 2 * m + width],
                       start=(m == 0), stop=False)
                for m in range(J // 4):
                    last = mm(conv_ps[:, 0:width], shift_lo[:, 2 * m:2 * m + 2, :],
                              et_hh[u][:, col - 2 * m:col - 2 * m + width], start=False, stop=(m == J // 4 - 1))
                return last

            def xbar_products():
                for c in range(KC):
                    last = mm(o_ps[:, 3, c:c + 1], w2c[:, P * c:P * (c + 1)], hbar[:, 0:1], start=True, stop=True)
                last.then_inc(mom_done, 1)
                pe.wait_ge(shift_set, 2)
                pe.wait_ge(pads_set, 2)
                conv(0, J - 2, 2).then_inc(pad_conv_done, 1)
                pe.wait_ge(mom_kept, 4)
                tr(o_ps[0:KC, 0, 0:P], xbar_col[:, :], ident_sb[:, :]).then_inc(mom_done, 1)
                pe.wait_ge(pad_conv_kept, 1)

            def xa_product():
                pe.wait_ge(aT_in, 16)
                for c in range(KC):
                    last = mm(sum_ps[0:E + 1, 0:ER], w2cT[:, c, :], aT_sb[:, c, :], start=(c == 0), stop=(c == KC - 1))
                last.then_inc(xa_done, 1)

            def ffn_products():
                pe.wait_ge(mom_kept, 5)
                for c in range(KC):
                    if c % 2 == 0:
                        pe.wait_ge(wT_in[c // 2], 16)
                    for n in range(2):
                        mm(o_ps[0:E + 1, n, :], w2cT[:, c, :], wT_sb[:, c, 512 * n:512 * (n + 1)], start=(c == 0), stop=False)
                pe.wait_ge(bfT_in, 16)
                for e in range(2):
                    for n in range(2):
                        last = mm(o_ps[0:E + 1, n, :], xaT_sb[:, e, :], bfT_sb[:, e, 512 * n:512 * (n + 1)], start=False, stop=(e == 1))
                last.then_inc(g_done, 1)

            def xbar_correlation():
                pe.wait_ge(hankel_in, 16 * KC)
                for c in range(KC):
                    mm(o_ps[0:1, 2, :], xbar_col_r[:, c:c + 1], hankel(c), start=(c == 0), stop=(c == KC - 1))
                for c in range(KC):
                    last = mm(o_ps[0:1, 3, 0:1], xbar_col[:, c:c + 1], xbar_col[:, c:c + 1], start=(c == 0), stop=(c == KC - 1))
                last.then_inc(acf_done, 1)

            def step(g, u, front, mid, back):
                a, b, c = 2 * g + u, 2 * g + u - 1, 2 * (g - 1) + u
                pb = 1 - u

                def tile_product(i):
                    if i == 0:
                        pe.wait_ge(hi_kept, 2 * c + 2)
                        pe.wait_ge(lo_kept, 2 * c + 2)
                        pe.wait_ge(xt_kept, c + 1)
                    ge(pe, oa_kept, NT * c + i - 1)
                    ge(pe, ov_kept, NT * c + i - 1)
                    cols = slice(P * i, P * (i + 1))
                    factors = ((u_hi[u][:, cols], w_hi), (u_lo[u][:, cols], w_hi), (u_hi[u][:, cols], w_lo),
                               (xT[u][:, P * (i // 4):P * (i // 4 + 1)], extra[i % 4]))
                    for n in range(2):
                        for f, (lhsT, rhs) in enumerate(factors):
                            last = mm(o_ps[:, 2 * (i % 2) + n, :], lhsT, rhs[:, 512 * n:512 * (n + 1)],
                                      start=(f == 0), stop=(f == len(factors) - 1))
                    last.then_inc(o_done, 1)

                def transpose_rows(hh):
                    if hh == 0:
                        ge(pe, rows_gathered[u], 16 * NT * (g + u))
                        if isinstance(g, int) and g + u == 0:
                            pe.wait_ge(rows0_split, 2)
                    ge(pe, et_back_kept, 2 * a + hh)
                    if hh == 0:
                        ge(pe, xt_kept, a - 1)
                    for i in range(4):
                        last = tr(et_ps[:, P * i:P * (i + 1)], gathered[u][:, 4 * hh + i, :], ident_sb[:, :])
                    last.then_inc(et_done, 1)

                def transpose_h():
                    ge(pe, hi_kept, 2 * b - 1)
                    ge(pe, lo_kept, 2 * b - 1)
                    wait_alone(pe, tanh_done, 2 * b + 2, pe_passed)
                    for i in range(NT):
                        last = tr(sum_ps[:, E * i:E * (i + 1)], hT[pb][0:E, P * i:P * (i + 1)], ident_sb[0:E, 0:E])
                    last.then_inc(h_done, 1)

                def moments_of(hh):
                    if hh == 0 and in_step(1, g, u):
                        pe.wait_ge(xa_kept, 4)
                    elif hh == 0:
                        ge(pe, hi_kept, 2 * b)
                        ge(pe, lo_kept, 2 * b)
                    else:
                        pe.wait_ge(h_ready, b + 1)
                    y = y_view(hh)
                    for i in range(4):
                        col = HALF * hh + P * i
                        last = mm(y[:, i, :], hT[pb][0:E + 1, col:col + P], moments[:, :], start=True, stop=True)
                    last.then_inc(y_done, 1)

                def conv_half(hh):
                    pe.wait_ge(et_kept, 2 * a + hh + 1)
                    pe.wait_ge(et_top_kept, 2 * a + hh + 1)
                    pe.wait_ge(et_back_kept, 2 * a + hh + 1)
                    ge(pe, shifts_added, 2 * a + hh)
                    conv(u, PAD + HALF * hh, HALF).then_inc(conv_done, 1)

                if back:
                    tile_product(0)
                if mid:
                    transpose_h()
                if front:
                    transpose_rows(0)
                if in_step(0, g, u):
                    xbar_products()
                if back:
                    tile_product(1)
                if mid:
                    moments_of(0)
                if front:
                    transpose_rows(1)
                if back:
                    tile_product(2)
                if mid:
                    moments_of(1)
                if back:
                    tile_product(3)
                if in_step(1, g, u):
                    xbar_correlation()
                    ffn_products()
                if front:
                    conv_half(0)
                if in_step(0, g, u):
                    xa_product()
                if back:
                    tile_product(4)
                    tile_product(5)
                if mid:
                    pe.wait_ge(u_ready, b + 1)
                    for hh, bank in enumerate((sum_ps, mix_ps)):
                        for i in range(4):
                            last = tr(bank[:, P * i:P * (i + 1)], u_row[:, 4 * hh + i, 0:2 * E], ident_sb[:, :])
                        last.then_inc(ut_done, 1)
                    pe.wait_ge(x_ready, b + 1)
                    ge(pe, et_back_kept, 2 * (a + front))
                    for hh in range(2):
                        last = tr(et_ps[:, P * hh:P * (hh + 1)],
                                  x_row[:, 4 * hh:4 * hh + 4, :].bitcast(F32).rearrange("p i x -> p (i x)"), ident_sb[:, :])
                    last.then_inc(xt_done, 1)
                if front:
                    conv_half(1)
                if back:
                    tile_product(6)
                    tile_product(7)

            def after_step0():
                pe.wait_ge(xa_kept, 2)
                for n in range(2):
                    last = tr(mix_ps[:, (E + 1) * n:(E + 1) * (n + 1)], xa_sb[:, P * n:P * (n + 1)], ident_sb[0:E + 1, 0:E + 1])
                last.then_inc(xa_done, 1)

            def after_step1():
                pe.wait_ge(w_set, 5)
                pe.wait_ge(acf_kept, 2)
                pe.wait_ge(rows_in, 48)

            pe.wait_ge(ones_set, 3)
            steps(pe, step, after_step0, after_step1)

            pe.wait_ge(flag_set, 1)
            need = pe.value_load(flag[0:1, 0:1], min_val=0, max_val=1)
            with pe.If(need != 0):
                ab0, ab1 = hT[0][:, :], hT[1][:, :]
                spec_w = gathered[1][:, :, :].rearrange("p i n -> p (i n)")
                left, right = (o_ps[:, n:n + 2, :].rearrange("p a n -> p (a n)") for n in (0, 2))
                table = obuf[:, :, :, :].rearrange("p a b n -> p (a b) n")

                def transpose_all():
                    for c in range(KC):
                        last = tr(right[:, P * c:P * (c + 1)], ab0[:, P * c:P * (c + 1)], ident_sb[:, :])
                    last.then_inc(g_pe, 1)

                def spectrum():
                    for m in range(KC):
                        for c in range(KC):
                            last = mm(left[:, P * m:P * (m + 1)], table[:, c, P * m:P * (m + 1)], ab1[:, P * c:P * (c + 1)],
                                      start=(c == 0), stop=(c == KC - 1))
                    last.then_inc(g_pe, 1)

                def rows_from(dst, lhsT):
                    for n in range(2):
                        for c in range(KC):
                            last = mm(dst[:, 512 * n:512 * (n + 1)], lhsT[:, P * c:P * (c + 1)], table[:, c, 512 * n:512 * (n + 1)],
                                      start=(c == 0), stop=(c == KC - 1))
                    last.then_inc(g_pe, 1)

                with pe.Fori(0, NSEQ * NT) as t:
                    pe.wait_ge(g_dve, 10 * t + 1)
                    tr(mix_ps[0:E + 1, 0:P], prod[:, 0, :], ident_sb[:, :]).then_inc(g_pe, 1)
                    pe.wait_ge(g_act, 7 * t + 1)
                    for n in range(2):
                        mm(left[:, 512 * n:512 * (n + 1)], g_hT[0:E + 1, 0:P], w2c[:, 512 * n:512 * (n + 1)], start=True, stop=True)
                    mm(sum_ps[:, 0:1], g_hT[0:E + 1, 0:P], w2mean[:, :], start=True, stop=True).then_inc(g_pe, 1)
                    pe.wait_ge(g_dve, 10 * t + 3)
                    transpose_all()
                    pe.wait_ge(g_act, 7 * t + 2)
                    pe.wait_ge(g_table_in, 96 * t + 16)
                    spectrum()
                    pe.wait_ge(g_act, 7 * t + 3)
                    pe.wait_ge(g_table_in, 96 * t + 32)
                    rows_from(right, spec_w)
                    pe.wait_ge(g_dve, 10 * t + 5)
                    transpose_all()
                    pe.wait_ge(g_act, 7 * t + 5)
                    pe.wait_ge(g_table_in, 96 * t + 64)
                    spectrum()
                    pe.wait_ge(g_dve, 10 * t + 6)
                    pe.wait_ge(g_table_in, 96 * t + 80)
                    rows_from(left, ab0)
                    pe.wait_ge(g_dve, 10 * t + 8)
                    transpose_all()
                    pe.wait_ge(g_act, 7 * t + 7)
                    for e in range(2):
                        for c in range(KC):
                            last = mm(sum_ps[:, P * e:P * (e + 1)], aT_sb[:, c, P * e:P * (e + 1)], ab1[:, P * c:P * (c + 1)],
                                      start=(c == 0), stop=(c == KC - 1))
                    last.then_inc(g_pe, 1)
                    pe.wait_ge(g_dve, 10 * t + 9)
                    pe.wait_ge(g_table_in, 96 * t + 96)
                    for n in range(2):
                        cols = slice(512 * n, 512 * (n + 1))
                        for c in range(KC):
                            mm(left[:, cols], ab1[:, P * c:P * (c + 1)], table[:, c, cols], start=(c == 0), stop=False)
                        for e in range(2):
                            mm(left[:, cols], spec_w[:, P * e:P * (e + 1)], bfT_sb[:, e, cols], start=False, stop=False)
                        last = mm(left[:, cols], g_ones[:, :], bias_row[:, cols], start=False, stop=True)
                    last.then_inc(g_pe, 1)



def kernel(**inputs):
    import concourse.bacc as bacc
    from concourse.bass_utils import run_bass_kernel_spmd

    x, w = inputs["x"], inputs["L0_ffn_W"]
    a, bf = inputs["L0_ffn_A"], inputs["L0_ffn_Bf"]
    by_rank = lambda v: np.ascontiguousarray(np.repeat(v, R).reshape(2, P).T)
    half = L // 2
    freq = np.concatenate([np.arange(half), np.arange(half)])
    freq[half] = half
    turn = np.outer(np.arange(L), freq) % L
    cosine = np.cos(2 * np.pi * np.minimum(turn, L - turn) / L)
    sine = np.sin(2 * np.pi * turn / L)
    dft = np.concatenate([cosine[:, :half + 1], sine[:, half + 1:]], 1)
    weight = np.where((np.arange(L) == 0) | (np.arange(L) == half), 1.0, 2.0) / L
    arrays = {
        "ids": np.ascontiguousarray(np.asarray(x).reshape(NSEQ * NT, P).T),
        "wte": inputs["L0_tok_wte"], "w1": inputs["L0_tok_w1"], "b1": inputs["L0_tok_b1"].reshape(E, 1),
        "w2": inputs["L0_tok_w2"], "b2": inputs["L0_tok_b2"].reshape(1, L),
        "wT": np.ascontiguousarray(w.T), "bias": inputs["L0_ffn_bias"].reshape(1, L),
        "aT": np.ascontiguousarray(a.reshape(ER, L).T),
        "bfT": np.ascontiguousarray(bf.transpose(0, 2, 1).reshape(ER, L)),
        "coeffs": by_rank(inputs["L0_ffn_coeffs"]), "scales": by_rank(inputs["L0_ffn_scales"]),
        "ident": np.eye(P, dtype=np.float32),
        "dft": dft.astype(np.float32),
        "idft": np.ascontiguousarray((dft * weight).T.astype(np.float32)),
        "acf": np.ascontiguousarray((cosine * weight).T.astype(np.float32)),
        "lags": np.tile(np.arange(L, dtype=np.float32), (P, 1)),
    }
    arrays = {n: np.ascontiguousarray(v) for n, v in arrays.items()}
    nc = bacc.Bacc("TRN2", target_bir_lowering=False, num_devices=1)
    args = {n: nc.dram_tensor(f"in_{n}", v.shape, mybir.dt.from_np(v.dtype), kind="ExternalInput").ap()
            for n, v in arrays.items()}
    out = nc.dram_tensor("out", (NSEQ, T, L), F32, kind="ExternalOutput").ap()
    tower_kernel(nc, out=out, **args)
    res = run_bass_kernel_spmd(nc, [{f"in_{n}": v for n, v in arrays.items()}], core_ids=[0])
    return res.results[0]["out"]
```

```python
import numpy as np
import concourse.bass as bass
from concourse import mybir
from concourse.alu_op_type import AluOpType as ALU
from contextlib import ExitStack

F32 = mybir.dt.float32
F32R = mybir.dt.float32r
I32 = mybir.dt.int32
U32 = mybir.dt.uint32
ACT = mybir.ActivationFunctionType
AX = mybir.AxisListType

P = 128
NSEQ, T, L = 16, 1024, 1024
E = 64
J = 16
VOCAB = 1024
NT = T // P
NE, R = 16, 16
ER = NE * R
KC = L // P
HALF = T // 2
EPS = 1e-5
GAP = 112.0
TOPK = 6
PAD = J
SPAN = PAD + T
XW = 32
NX = 8



def ge(eng, sem, count):
    if not isinstance(count, int) or count > 0:
        eng.wait_ge(sem, count)


def wait_alone(eng, sem, count, passed):
    eng.wait_ge(sem, count)
    if not isinstance(count, int):
        eng.sem_inc(passed, 1)


def tower_kernel(nc, ids, wte, w1, b1, w2, b2, wT, bias, aT, bfT, coeffs, scales,
                 ident, dft, idft, acf, lags, out, force_general=False):
    ctx = ExitStack()
    with ctx:
        def sb(name, shape, dt=F32):
            return ctx.enter_context(nc.sbuf_tensor(name, shape, dt))

        def ps(name, shape):
            return ctx.enter_context(nc.psum_tensor(name, shape, F32))

        def sem(name):
            return ctx.enter_context(nc.semaphore(name))

        xbar_twice = nc.dram_tensor("xbar_twice", (2 * L,), F32, kind="Internal").ap()

        ids_sb = sb("ids_sb", [P, NSEQ * NT], I32)
        ident_sb = sb("ident_sb", [P, P])
        shift_hi = sb("shift_hi", [P, J, E], F32R)
        shift_lo = sb("shift_lo", [P, J // 2, E], F32R)
        b1_col = sb("b1_col", [P, 1])
        hbar = sb("hbar", [E + 1, P])
        w2c = sb("w2c", [E + 1, L])
        w2mean = sb("w2mean", [E + 1, 1])
        moments = sb("moments", [E + 1, E + 3])
        moments_two = sb("moments_two", [P, 2 * (E + 3)])
        last_moments = sb("last_moments", [P, 3])
        w_hi = sb("w_hi", [P, L], F32R)
        w_lo = sb("w_lo", [P, L], F32R)
        extra = [sb(f"extra{i}", [P, L], F32R) for i in range(4)]
        aT_sb = sb("aT_sb", [P, KC, ER])
        bfT_sb = sb("bfT_sb", [P, 2, L])
        bias_row = sb("bias_row", [1, L])
        er_w = sb("er_w", [P, 2])
        h_all = sb("h_all", [P, NSEQ * NT * E])

        idx_now = [sb(f"idx_now{p}", [P, NT], I32) for p in range(2)]
        gathered = [sb(f"gathered{p}", [P, 2 * NT, E]) for p in range(2)]
        et_hl = [sb(f"et_hl{p}", [P, SPAN], F32R) for p in range(2)]
        et_hh = [sb(f"et_hh{p}", [P, SPAN + 8], F32R) for p in range(2)]
        hT = [sb(f"hT{p}", [P, T]) for p in range(2)]
        u_hi = [sb(f"u_hi{p}", [P, T], F32R) for p in range(2)]
        u_lo = [sb(f"u_lo{p}", [P, T], F32R) for p in range(2)]
        xT = [sb(f"xT{p}", [P, 2 * P], F32R) for p in range(2)]
        a_sb = [sb(f"a_sb{p}", [P, NT]) for p in range(2)]
        mean_sb = [sb(f"mean_sb{p}", [P, NT]) for p in range(2)]
        u_rows = sb("u_rows", [P, NT * (2 * E + 1)])
        h_row = u_rows[:, 0:NT * (E + 1)].rearrange("p (i n) -> p i n", i=NT)
        bh_row = u_rows[:, NT * (E + 1):].rearrange("p (i e) -> p i e", i=NT)
        odd = sb("odd", [P, T + 1])
        x_row = sb("x_row", [P, NT, XW], F32R)
        prod = sb("prod", [P, NT, E + 1])
        quad = sb("quad", [P, NT])
        var = sb("var", [P, NT])
        lin = sb("lin", [P, NT])
        cert = sb("cert", [P, NT])
        cert_max = sb("cert_max", [P, NT])
        var_eps = sb("var_eps", [P, NT])
        inv_std = sb("inv_std", [P, NT])
        a_sq = sb("a_sq", [P, NT])
        var2 = sb("var2", [P, NT])
        var2_eps = sb("var2_eps", [P, NT])
        beta = sb("beta", [P, NT])
        inv_a = sb("inv_a", [P, NT])
        minus_half = sb("minus_half", [P, NT])
        obuf = sb("obuf", [P, 4, 2, L])
        verdict = sb("verdict", [P, 8])
        flag = sb("flag", [1, 1], I32)
        pad_col = sb("pad_col", [E, 1])
        xbar_col = sb("xbar_col", [P, KC])
        xbar_col_r = sb("xbar_col_r", [P, KC], F32R)
        g_ones = sb("g_ones", [1, P])
        g_row = sb("g_row", [P, 32])
        g_idx = sb("g_idx", [P, 8], U32)

        g_stats = sb("g_stats", [P, 12])
        g_mv = sb("g_mv", [P, 2])

        wT_sb = h_all[:, :].rearrange("p (c n) -> p c n", c=KC)
        w1_ld = obuf[:, 0, 0, :].rearrange("p (j n) -> p j n", j=J)
        w2cT = obuf[:, 0, 1, 0:KC * (E + 1)].rearrange("p (c n) -> p c n", c=KC)
        xa_sb = obuf[0:E + 1, 1, 0, 0:ER]
        xaT_sb = obuf[:, 1, 0, ER:ER + 2 * (E + 1)].rearrange("p (c n) -> p c n", c=2)
        er_ld = obuf[:, 1, 0, 512:516]
        xbar_rows = xT[0][0:KC, 0:P]
        b_hi, b_lo = u_hi[1][E:E + 1, :], u_lo[1][E:E + 1, :]
        bias_hi, bias_lo = u_hi[1][0:1, :], u_lo[1][0:1, :]
        g_hi, g_lo = u_hi[1][96:97, :], u_lo[1][96:97, :]

        def hankel(c):
            tile = (P * c + 512) > L
            return extra[tile][:, P * c - 512 * tile:P * c - 512 * tile + 512]

        g_hT = odd[:, 0:T]

        o_ps = ps("o_ps", [P, 4, 512])
        conv_ps = ps("conv_ps", [P, 512])
        et_ps = ps("et_ps", [P, 512])
        sum_ps = ps("sum_ps", [P, 512])
        mix_ps = ps("mix_ps", [P, 512])

        def tiles_of(seq, odd_tiles):
            return seq.rearrange("p (j two n) -> p j two n", two=2, n=P)[:, :, odd_tiles, :]

        def pair_bank(bank, odd_tiles):
            return bank[E * odd_tiles:E * odd_tiles + E, :].rearrange("p (j n) -> p j n", n=P)

        def y_view(hh):
            return (mix_ps, sum_ps)[hh][:, 0:4 * (E + 3)].rearrange("p (j two n) -> p j two n", j=2, two=2)

        def in_pairs(rows):
            if len(rows.shape) == 2:
                return rows.rearrange("p (two j) -> p j two", two=2)
            return rows.rearrange("p (two j) n -> p j two n", two=2)

        ids_in, pad_in, w1_in, b1_in, consts_in, w2_in, small_in, aT_in, bfT_in, hankel_in = (
            sem(n) for n in ("ids_in", "pad_in", "w1_in", "b1_in", "consts_in", "w2_in", "small_in", "aT_in", "bfT_in", "hankel_in"))
        wT_in = [sem(f"wT_in{n}") for n in range(KC // 2)]
        zeros_set = sem("zeros_set")
        pads_hi = sem("pads_hi")
        pads_set = sem("pads_set")
        shift_hi_set = sem("shift_hi_set")
        shift_set = sem("shift_set")
        pad_conv_done = sem("pad_conv_done")
        pad_conv_kept = sem("pad_conv_kept")
        w2_sum = sem("w2_sum")
        w2_mean = sem("w2_mean")
        w2_centred = sem("w2_centred")
        w2T_done = sem("w2T_done")
        w2T_kept = sem("w2T_kept")
        ones_set = sem("ones_set")
        blocks_zeroed = sem("blocks_zeroed")
        blocks_set = sem("blocks_set")
        hbar_set = sem("hbar_set")
        mom_done = sem("mom_done")
        mom_kept = sem("mom_kept")
        xbar_step = sem("xbar_step")
        xbar_stored = sem("xbar_stored")
        xa_done = sem("xa_done")
        xa_kept = sem("xa_kept")
        g_done = sem("g_done")
        w_hi_set = sem("w_hi_set")
        extra_zeroed = sem("extra_zeroed")
        w_set = sem("w_set")
        g_hi_set = sem("g_hi_set")
        row0_in, rows_in = sem("row0_in"), sem("rows_in")
        acf_done = sem("acf_done")
        acf_kept = sem("acf_kept")
        idx_ready = sem("idx_ready")
        rows_gathered = [sem(f"rows_gathered{p}") for p in range(2)]
        et_done = sem("et_done")
        et_hi_kept = sem("et_hi_kept")
        et_lo_kept = sem("et_lo_kept")
        et_top_kept = sem("et_top_kept")
        et_back_kept = sem("et_back_kept")
        conv_done = sem("conv_done")
        odd_kept = sem("odd_kept")
        shifts_added = sem("shifts_added")
        tanh_done = sem("tanh_done")
        h_done = sem("h_done")
        h_ready = sem("h_ready")
        h_saved = sem("h_saved")
        y_done = sem("y_done")
        prod_ready = sem("prod_ready")
        quad_ready = sem("quad_ready")
        var_ready = sem("var_ready")
        cert_step = sem("cert_step")
        scal_step = sem("scal_step")
        u_ready = sem("u_ready")
        x_step = sem("x_step")
        x_ready = sem("x_ready")
        h_hi_kept = sem("h_hi_kept")
        h_lo_kept = sem("h_lo_kept")
        ut_done = sem("ut_done")
        hi_kept = sem("hi_kept")
        lo_kept = sem("lo_kept")
        xt_done = sem("xt_done")
        xt_kept = sem("xt_kept")
        o_done = sem("o_done")
        oa_kept = sem("oa_kept")
        ov_kept = sem("ov_kept")
        stored = [sem(f"stored{q}") for q in range(4)]
        v_dve = sem("v_dve")
        v_pool = sem("v_pool")
        flag_set = sem("flag_set")
        g_pe, g_dve, g_act, g_pool = sem("g_pe"), sem("g_dve"), sem("g_act"), sem("g_pool")
        g_link = sem("g_link")
        pool_passed, sp_passed, dve_passed = (
            sem(f"{eng}_passed") for eng in ("pool", "sp", "dve"))
        g_table_in, g_stored = sem("g_table_in"), sem("g_stored")

        out_pairs = out.rearrange("s (q i p) o -> (s q) p i o", i=2, p=P)
        out_tiles = out.rearrange("s (i p) o -> (s i) p o", p=P)

        FIRST = 4

        def in_step(k, g, u):
            return isinstance(g, int) and 2 * g + u == k

        def steps(eng, step, after_step0, after_step1):
            for k in range(FIRST):
                step(k // 2, k % 2, True, k >= 1, k >= 2)
                if k == 0:
                    after_step0()
                if k == 1:
                    after_step1()
            with eng.Fori(FIRST // 2, NSEQ // 2) as g:
                step(g, 0, True, True, True)
                step(g, 1, True, True, True)
            for k in range(NSEQ, NSEQ + 2):
                step(k // 2, k % 2, False, k <= NSEQ, True)

        block = ctx.enter_context(nc.Block())

        @block.sync
        def _(sp):
            sp.dma_start(ids_sb[:, :], ids).then_inc(ids_in, 16)
            sp.dma_start(w2c[0:E, :], w2).then_inc(w2_in, 16)
            sp.dma_start(w2c[E:E + 1, :], b2).then_inc(w2_in, 16)
            sp.dma_start(ident_sb[:, :], ident).then_inc(consts_in, 16)
            for half in range(2):
                sp.dma_start(b1_col[E * half:E * half + E, :], b1).then_inc(b1_in, 16)
            for half in range(2):
                sp.dma_start(w1_ld[E * half:E * half + E], w1.rearrange("(j e) n -> e j n", e=E)).then_inc(w1_in, 16)
            sp.dma_start(pad_col[:, :], wte[VOCAB:VOCAB + 1, :].rearrange("a e -> e a")).then_inc(pad_in, 16)
            sp.dma_start(er_ld[:, 0:2], coeffs).then_inc(small_in, 16)
            sp.dma_start(er_ld[:, 2:4], scales).then_inc(small_in, 16)
            sp.dma_start(bias_row[:, :], bias).then_inc(small_in, 16)
            sp.wait_ge(rows_gathered[0], 16 * NT)
            sp.dma_start(aT_sb[:, :, :], aT.rearrange("(c p) n -> p c n", p=P)).then_inc(aT_in, 16)

            def load_wT(half):
                for c in range(half * KC // 2, (half + 1) * KC // 2, 2):
                    sp.dma_start(wT_sb[:, c:c + 2, :], wT[P * c:P * (c + 2), :].rearrange("(c p) n -> p c n", p=P)).then_inc(wT_in[c // 2], 16)

            load_wT(0)
            sp.wait_ge(mom_kept, 5)
            for n in range(2):
                sp.dma_start(xbar_twice[L * n:L * (n + 1)].rearrange("(c p) -> c p", p=P), xbar_rows.bitcast(F32)).then_inc(xbar_stored, 16)
            sp.wait_ge(xbar_stored, 32)
            for n in range(2):
                width = L - P * n
                sp.dma_start(extra[n][:, 0:width].bitcast(F32), bass.AP(xbar_twice.tensor, 512 * n + 1, [[1, P], [1, width]])).then_inc(hankel_in, 16)
            load_wT(1)
            sp.dma_start(bfT_sb[:, :, :], bfT.rearrange("(c p) n -> p c n", p=P)).then_inc(bfT_in, 16)
            sp.wait_ge(extra_zeroed, 1)
            sp.wait_ge(w_set, 3)
            for n, row in ((0, b_hi), (1, b_lo), (5, bias_hi), (6, bias_lo), (7, bias_hi)):
                sp.dma_start(extra[0][n:n + 1, :].bitcast(F32), row.bitcast(F32)).then_inc(row0_in, 16)
            sp.wait_ge(w_set, 4)
            for n, row in ((2, g_hi), (3, g_lo), (4, g_hi)):
                sp.dma_start(extra[0][n:n + 1, :].bitcast(F32), row.bitcast(F32)).then_inc(row0_in, 16)
            sp.wait_ge(row0_in, 16 * NX)
            for i in range(1, 4):
                sp.dma_start(extra[i][XW * i:XW * i + NX, :].bitcast(F32), extra[0][0:NX, :].bitcast(F32)).then_inc(rows_in, 16)

            def step(g, u, front, mid, back):
                if back:
                    c = 2 * (g - 1) + u
                    last = not front and not mid
                    for q in range(3 if last else 4):
                        sp.wait_ge(oa_kept, NT * c + 2 * q + 2)
                        sp.wait_ge(ov_kept, NT * c + 2 * q + 2)
                        sp.dma_start(out_pairs[bass.ds(4 * c + q, 1)].rearrange("a p i o -> (a p) i o"),
                                     obuf[:, q, :, :]).then_inc(stored[q], 16)
                    if last:
                        sp.wait_ge(oa_kept, NT * c + 7)
                        sp.wait_ge(ov_kept, NT * c + 7)
                        sp.dma_start(out_tiles[NT * c + 6], obuf[:, 3, 0, :]).then_inc(stored[3], 16)
                        sp.wait_ge(oa_kept, NT * c + 8)
                        sp.dma_start(out_tiles[NT * c + 7][:, 0:512], obuf[:, 3, 1, 0:512]).then_inc(stored[3], 16)
                        sp.wait_ge(ov_kept, NT * c + 8)
                        sp.dma_start(out_tiles[NT * c + 7][:, 512:L], obuf[:, 3, 1, 512:L]).then_inc(stored[3], 16)

            steps(sp, step, lambda: None, lambda: None)
            for q in range(4):
                sp.wait_ge(stored[q], 16 * (NSEQ + 2 * (q == 3)))

            sp.wait_ge(flag_set, 1)
            need = sp.value_load(flag[0:1, 0:1], min_val=0, max_val=1)
            table = obuf[:, :, :, :].rearrange("p a b n -> p (a b) n")
            with sp.If(need != 0):
                with sp.Fori(0, NSEQ * NT) as t:
                    for n, (src, used, count) in enumerate((
                            (dft, g_dve, 10 * t + 1), (acf, g_pe, 11 * t + 4), (lags, g_pe, 11 * t + 5),
                            (dft, g_dve, 10 * t + 5), (idft, g_pe, 11 * t + 7), (wT, g_pe, 11 * t + 8))):
                        sp.wait_ge(used, count)
                        dst, rows = (table[:, 0, :], src) if n == 2 else (table, src.rearrange("(c p) n -> p c n", p=P))
                        sp.dma_start(dst, rows).then_inc(g_table_in, 16)
                        wait_alone(sp, g_table_in, 96 * t + 16 * n + 16, sp_passed)
                    sp.wait_ge(g_dve, 10 * t + 10)
                    sp.dma_start(out_tiles[bass.ds(t, 1)].rearrange("a p o -> (a p) o"), g_hT[:, :]).then_inc(g_stored, 16)
                    wait_alone(sp, g_stored, 16 * t + 16, sp_passed)

        @block.gpsimd
        def _(pool):
            def gather(s, p, uses):
                ge(pool, et_done, uses)
                pool.tensor_copy(idx_now[p][:, :], ids_sb[:, bass.ds(NT * s, NT)]).then_inc(idx_ready, 1)
                wait_alone(pool, idx_ready, s + 1, pool_passed)

            def gather_rows(p, i):
                pool.indirect_dma_start(
                    gathered[p][:, i, :], None, wte,
                    bass.IndirectOffsetOnAxis(ap=idx_now[p][:, i:i + 1].bitcast(U32), axis=0),
                ).then_inc(rows_gathered[p], 16)

            pool.wait_ge(ids_in, 16)
            gather(0, 0, 0)
            for i in range(NT):
                gather_rows(0, i)
            pool.memset(x_row[:, :, :].bitcast(F32), 0.0)
            pool.memset(minus_half[:, :], -0.5)
            pool.memset(g_ones[:, :], 1.0)
            pool.memset(cert_max[:, :], -3.0e38)
            pool.memset(h_row[:, :, E:E + 1], 2.0).then_inc(zeros_set, 1)
            pool.wait_ge(zeros_set, 1)
            pool.memset(x_row[:, :, 0:2].bitcast(F32), 1.0).then_inc(zeros_set, 1)

            def step(g, u, front, mid, back, last=False):
                a, b = 2 * g + u, 2 * g + u - 1
                more = front and not last
                if more:
                    gather(a + 1, 1 - u, a)
                    for i in range(NT // 2):
                        gather_rows(1 - u, i)
                if in_step(1, g, u):
                    pool.wait_ge(acf_done, 1)
                    for i in range(4):
                        last_fill = pool.memset(extra[i][:, :].bitcast(F32), 0.0)
                    last_fill.then_inc(extra_zeroed, 1)
                if mid:
                    pb = 1 - u
                    wait_alone(pool, var_ready, b + 1, pool_passed)
                    pool.tensor_scalar(var_eps[:, :], var[:, :], EPS, None, ALU.add).then_inc(scal_step, 1)
                    wait_alone(pool, scal_step, 7 * b + 1, pool_passed)
                    pool.tensor_tensor(inv_std[:, :], var_eps[:, :], minus_half[:, :], ALU.pow).then_inc(scal_step, 1)
                    wait_alone(pool, scal_step, 7 * b + 2, pool_passed)
                    pool.tensor_scalar(a_sb[pb][:, :], inv_std[:, :], 1.0, None, ALU.add).then_inc(scal_step, 1)
                    wait_alone(pool, scal_step, 7 * b + 3, pool_passed)
                    pool.tensor_tensor(a_sq[:, :], a_sb[pb][:, :], a_sb[pb][:, :], ALU.mult).then_inc(scal_step, 1)
                    wait_alone(pool, scal_step, 7 * b + 4, pool_passed)
                    pool.tensor_tensor(var2[:, :], a_sq[:, :], var[:, :], ALU.mult).then_inc(scal_step, 1)
                    wait_alone(pool, scal_step, 7 * b + 5, pool_passed)
                    pool.tensor_scalar(var2_eps[:, :], var2[:, :], EPS, None, ALU.add).then_inc(scal_step, 1)
                    wait_alone(pool, scal_step, 7 * b + 6, pool_passed)
                    pool.tensor_tensor(beta[:, :], var2_eps[:, :], minus_half[:, :], ALU.pow).then_inc(scal_step, 1)
                    if in_step(1, g, u):
                        pool.wait_ge(g_done, 1)
                    pool.wait_ge(h_ready, b + 1)
                    pool.tensor_copy(h_all[:, bass.ds(NT * E * b, NT * E)].rearrange("p (i e) -> p i e", i=NT),
                                     h_row[:, :, 0:E]).then_inc(h_saved, 1)
                if more:
                    for i in range(NT // 2, NT):
                        gather_rows(1 - u, i)

            for k in range(FIRST):
                step(k // 2, k % 2, True, k >= 1, k >= 2)
            with pool.Fori(FIRST // 2, NSEQ // 2 - 1) as g:
                step(g, 0, True, True, True)
                step(g, 1, True, True, True)
            for k in range(NSEQ - 2, NSEQ + 2):
                step(k // 2, k % 2, k < NSEQ, k <= NSEQ, True, last=k == NSEQ - 1)

            pool.wait_ge(v_dve, 1)
            pool.partition_all_reduce(verdict[:, 4:5], verdict[:, 3:4], P, bass.bass_isa.ReduceOp.max).then_inc(v_pool, 1)

            pool.wait_ge(flag_set, 1)
            need = pool.value_load(flag[0:1, 0:1], min_val=0, max_val=1)
            with pool.If(need != 0):
                with pool.Fori(0, NSEQ * NT) as t:
                    for n in range(2):
                        pool.wait_ge(g_dve, 10 * t + (2, 7)[n])
                        pool.tensor_tensor(g_row[:, 4 * n + 1:4 * n + 2], g_row[:, 4 * n:4 * n + 1],
                                           minus_half[:, 0:1], ALU.pow).then_inc(g_pool, 1)

        @block.scalar
        def _(act):
            act.wait_ge(b1_in, 32)
            nc.scalar.activation(hbar[0:E, :], b1_col[0:E, 0:1].to_broadcast([E, P]), ACT.Tanh).then_inc(hbar_set, 1)
            act.wait_ge(w2T_done, 1)
            for n, bank in enumerate((sum_ps, mix_ps)):
                nc.scalar.copy(w2cT[:, 4 * n:4 * n + 4, :],
                               bank[:, 0:4 * (E + 1)].rearrange("p (c n) -> p c n", c=4)).then_inc(w2T_kept, 1)

            act.wait_ge(w1_in, 32)
            nc.scalar.copy(shift_hi[:, :, :], w1_ld).then_inc(shift_hi_set, 1)
            def tile_out(c, pc, i):
                q = i // 2
                if i % 2 == 0:
                    ge(act, stored[q], 16 * c)
                act.wait_ge(o_done, NT * c + i + 1)
                nc.scalar.activation(obuf[:, q, i % 2, 0:512], o_ps[:, 2 * (i % 2), :], ACT.Identity,
                                     bias=mean_sb[pc][:, i:i + 1], scale=a_sb[pc][:, i:i + 1]).then_inc(oa_kept, 1)

            def step(g, u, front, mid, back):
                a, b, c = 2 * g + u, 2 * g + u - 1, 2 * (g - 1) + u
                pb = 1 - u

                def keep_et_hi():
                    act.wait_ge(et_done, a + 1)
                    for odd_tiles in range(2):
                        nc.scalar.copy(tiles_of(et_hl[u][0:E, PAD:SPAN], odd_tiles),
                                       pair_bank(et_ps, odd_tiles)).then_inc(et_hi_kept, 1)

                def keep_et_back():
                    act.wait_ge(et_hi_kept, 2 * a + 2)
                    nc.scalar.copy(et_hh[u][E:P, PAD + 8:PAD + 8 + T], et_hl[u][0:E, PAD:SPAN].bitcast(F32)).then_inc(et_back_kept, 1)

                def keep_odd(hh):
                    act.wait_ge(conv_done, 2 * a + hh + 1)
                    ge(act, shifts_added, 2 * a + hh)
                    n = HALF - hh
                    nc.scalar.copy(odd[0:E, HALF * hh + 1:HALF * hh + 1 + n], conv_ps[E:P, 0:n]).then_inc(odd_kept, 1)

                def take_tanh(hh):
                    act.wait_ge(shifts_added, 2 * a + hh + 1)
                    rows = slice(E * hh, E * (hh + 1))
                    nc.scalar.activation(hT[u][rows, 0:HALF], hT[u][rows, 0:HALF], ACT.Tanh,
                                         bias=b1_col[rows, 0:1]).then_inc(tanh_done, 1)

                if back:
                    tile_out(c, u, 0)
                if mid:
                    act.wait_ge(h_done, b + 1)
                    ge(act, h_saved, b)
                    nc.scalar.copy(in_pairs(h_row[:, :, 0:E]),
                                   sum_ps[:, :].rearrange("p (j two e) -> p j two e", two=2, e=E)).then_inc(h_ready, 1)
                if front:
                    keep_et_hi()
                if back:
                    tile_out(c, u, 1)
                if front:
                    keep_et_back()
                if in_step(0, g, u):
                    act.wait_ge(pad_conv_done, 1)
                    nc.scalar.copy(odd[0:E, 0:1], conv_ps[E:P, 0:1]).then_inc(pad_conv_kept, 1)
                if back:
                    tile_out(c, u, 2)
                    tile_out(c, u, 3)
                if mid:
                    act.wait_ge(tanh_done, 2 * b + 2)
                    nc.scalar.copy(u_hi[pb][0:E, 0:HALF], hT[pb][0:E, 0:HALF])
                    nc.scalar.copy(hT[pb][E:P, HALF:T].bitcast(F32R), hT[pb][E:P, 0:HALF])
                    nc.scalar.copy(u_hi[pb][0:E, HALF:T], hT[pb][E:P, 0:HALF]).then_inc(h_hi_kept, 1)
                if in_step(1, g, u):
                    act.wait_ge(g_done, 1)
                    nc.scalar.copy(g_hi, o_ps[E:E + 1, 0:2, :].rearrange("p a n -> p (a n)")).then_inc(g_hi_set, 1)
                if front:
                    keep_odd(0)
                if back:
                    tile_out(c, u, 4)
                if front:
                    take_tanh(0)
                if back:
                    tile_out(c, u, 5)
                if back and not front:
                    tile_out(c, u, 6)
                if mid:
                    act.wait_ge(ut_done, b + 1)
                    for odd_tiles in range(2):
                        nc.scalar.copy(tiles_of(u_hi[pb][E:P, :], odd_tiles), pair_bank(sum_ps, odd_tiles)).then_inc(hi_kept, 1)
                    act.wait_ge(xt_done, b + 1)
                    nc.scalar.copy(xT[pb][:, :], et_ps[:, 0:2 * P]).then_inc(xt_kept, 1)
                if front:
                    keep_odd(1)
                if front:
                    take_tanh(1)
                if back and front:
                    tile_out(c, u, 6)
                if back:
                    tile_out(c, u, 7)

            steps(act, step, lambda: None, lambda: None)

            act.wait_ge(flag_set, 1)
            need = act.value_load(flag[0:1, 0:1], min_val=0, max_val=1)
            with act.If(need != 0):
                with act.Fori(0, NSEQ * NT) as t:
                    act.wait_ge(g_pe, 11 * t + 1)
                    nc.scalar.copy(g_hT[0:E + 1, 0:P], mix_ps[0:E + 1, 0:P]).then_inc(g_act, 1)
                    act.wait_ge(g_pe, 11 * t + 3)
                    nc.scalar.copy(hT[1][:, :], o_ps[:, 2:4, :].rearrange("p a n -> p (a n)")).then_inc(g_act, 1)
                    act.wait_ge(g_pe, 11 * t + 4)
                    spec = gathered[0][:, :, :].rearrange("p i n -> p (i n)")
                    nc.scalar.copy(spec, o_ps[:, 0:2, :].rearrange("p a n -> p (a n)"))
                    nc.scalar.activation(gathered[1][:, :, :].rearrange("p i n -> p (i n)"),
                                         o_ps[:, 0:2, :].rearrange("p a n -> p (a n)"), ACT.Square).then_inc(g_act, 1)
                    act.wait_ge(g_dve, 10 * t + 4)
                    nc.scalar.activation(g_row[:, 16:16 + TOPK], g_row[:, 8:8 + TOPK], ACT.Exp, bias=g_row[:, 3:4],
                                         accum_out=g_row[:, 2:3]).then_inc(g_act, 1)
                    act.wait_ge(g_pe, 11 * t + 6)
                    nc.scalar.copy(hT[1][:, :], o_ps[:, 2:4, :].rearrange("p a n -> p (a n)")).then_inc(g_act, 1)
                    act.wait_ge(g_pe, 11 * t + 7)
                    nc.scalar.copy(gathered[1][:, :, :].rearrange("p i n -> p (i n)"),
                                   o_ps[:, 0:2, :].rearrange("p a n -> p (a n)")).then_inc(g_act, 1)
                    act.wait_ge(g_pe, 11 * t + 9)
                    nc.scalar.copy(hT[1][:, :], o_ps[:, 2:4, :].rearrange("p a n -> p (a n)")).then_inc(g_act, 1)

        @block.vector
        def _(dve):
            nc.vector.memset(hbar[E:E + 1, :], 1.0).then_inc(ones_set, 1)
            nc.vector.memset(moments_two[:, :], 0.0).then_inc(blocks_zeroed, 1)
            dve.wait_ge(w2_in, 32)
            nc.vector.reduce_sum(w2mean[:, :], w2c[:, :], AX.X).then_inc(w2_sum, 1)
            dve.wait_ge(w2_sum, 1)
            nc.vector.tensor_scalar(w2mean[:, :], w2mean[:, :], 1.0 / L, None, ALU.mult).then_inc(w2_mean, 1)
            dve.wait_ge(w2_mean, 1)
            nc.vector.tensor_scalar(w2c[:, :], w2c[:, :], w2mean[:, 0:1], None, ALU.subtract).then_inc(w2_centred, 1)
            dve.wait_ge(pad_in, 16)
            for p in range(2):
                nc.vector.tensor_copy(et_hh[p][0:E, 0:PAD], pad_col[:, 0:1].to_broadcast([E, PAD]))
                nc.vector.tensor_copy(et_hh[p][E:P, 0:PAD + 8], pad_col[:, 0:1].to_broadcast([E, PAD + 8]))
                nc.vector.tensor_copy(et_hl[p][0:E, 0:PAD], pad_col[:, 0:1].to_broadcast([E, PAD])).then_inc(pads_hi, 1)
            dve.wait_ge(pads_hi, 2)
            for p in range(2):
                nc.vector.tensor_tensor(et_hl[p][E:P, 0:PAD], pad_col[:, 0:1].to_broadcast([E, PAD]),
                                        et_hl[p][0:E, 0:PAD].bitcast(F32), ALU.subtract).then_inc(pads_set, 1)
            dve.wait_ge(mom_done, 1)
            nc.vector.tensor_copy(moments[:, E + 1:E + 2], w2mean[:, :])
            nc.vector.tensor_scalar(moments[:, 0:E + 1], o_ps[0:E + 1, 0, 0:E + 1], 1.0 / L, None,
                                    ALU.mult).then_inc(mom_kept, 1)
            dve.wait_ge(mom_done, 2)
            nc.vector.tensor_copy(moments[:, E + 2:E + 3], o_ps[0:E + 1, 1, 0:1]).then_inc(mom_kept, 1)
            dve.wait_ge(shift_hi_set, 1)
            for half in range(2):
                rows, js = slice(E * half, E * half + E), slice(J // 2 * half, J // 2 * (half + 1))
                nc.vector.tensor_tensor(shift_lo[rows, :, :], w1_ld[rows, js, :], shift_hi[rows, js, :].bitcast(F32),
                                        ALU.subtract).then_inc(shift_set, 1)
            dve.wait_ge(mom_done, 3)
            nc.vector.tensor_copy(last_moments[:, :], o_ps[:, 2, 1:4])
            nc.vector.tensor_copy(verdict[:, 0:1], o_ps[:, 2, 0:1]).then_inc(mom_kept, 1)
            dve.wait_ge(mom_kept, 3)
            dve.wait_ge(blocks_zeroed, 1)
            for half in range(2):
                nc.vector.tensor_copy(moments_two[E * half:E * half + E, (E + 3) * half:(E + 3) * (half + 1)],
                                      moments[0:E, :]).then_inc(blocks_set, 1)
            dve.wait_ge(mom_done, 4)
            dve.wait_ge(w2T_kept, 2)
            nc.vector.tensor_tensor(prod[:, :, :], w2cT, o_ps[:, 3, 0:E + 1].unsqueeze(1).to_broadcast([P, KC, E + 1]),
                                    ALU.mult).then_inc(xbar_step, 1)
            dve.wait_ge(xbar_step, 1)
            nc.vector.tensor_reduce(xbar_col[:, :], prod[:, :, :], AX.X, ALU.add).then_inc(mom_kept, 1)
            dve.wait_ge(mom_kept, 4)
            nc.vector.tensor_copy(xbar_col_r[:, :], xbar_col[:, :]).then_inc(xbar_step, 1)

            def tile_out(c, pc, i):
                q = i // 2
                if i % 2 == 0:
                    ge(dve, stored[q], 16 * c)
                dve.wait_ge(o_done, NT * c + i + 1)
                nc.vector.tensor_scalar(obuf[:, q, i % 2, 512:L], o_ps[:, 2 * (i % 2) + 1, :], a_sb[pc][:, i:i + 1],
                                        mean_sb[pc][:, i:i + 1], ALU.mult, ALU.add).then_inc(ov_kept, 1)

            def keep_xbar_rows():
                dve.wait_ge(mom_done, 5)
                nc.vector.tensor_copy(xbar_rows, o_ps[0:KC, 0, 0:P]).then_inc(mom_kept, 1)

            def keep_xa():
                dve.wait_ge(small_in, 48)
                nc.vector.tensor_tensor(er_w[:, :], er_ld[:, 0:2], er_ld[:, 2:4], ALU.mult).then_inc(xa_kept, 1)
                dve.wait_ge(xa_done, 1)
                nc.vector.tensor_copy(xa_sb, sum_ps[0:E + 1, 0:ER]).then_inc(xa_kept, 1)

            def least_gap():
                dve.wait_ge(acf_done, 1)
                nc.vector.reduce_max(verdict[0:1, 1:2], o_ps[0:1, 2, :], AX.X).then_inc(acf_kept, 1)
                dve.wait_ge(acf_kept, 1)
                nc.vector.scalar_tensor_tensor(verdict[0:1, 2:3], o_ps[0:1, 3, 0:1], 1.0 - 1.0 / 512, verdict[0:1, 1:2],
                                               ALU.mult, ALU.subtract).then_inc(acf_kept, 1)

            def weight_halves():
                nc.vector.tensor_copy(b_hi, w2c[E:E + 1, :])
                nc.vector.tensor_copy(w_hi[0:E, :], w2c[0:E, :]).then_inc(w_hi_set, 1)
                dve.wait_ge(w_hi_set, 1)
                nc.vector.tensor_tensor(w_lo[0:E, :], w2c[0:E, :], w_hi[0:E, :].bitcast(F32), ALU.subtract).then_inc(w_set, 1)
                nc.vector.tensor_tensor(b_lo, w2c[E:E + 1, :], b_hi.bitcast(F32), ALU.subtract).then_inc(w_set, 1)
                nc.vector.tensor_copy(bias_hi, bias_row[:, :]).then_inc(w_hi_set, 1)
                dve.wait_ge(w_hi_set, 2)
                nc.vector.tensor_tensor(bias_lo, bias_row[:, :], bias_hi.bitcast(F32), ALU.subtract).then_inc(w_set, 1)

            gw = o_ps[0:E, 0:2, :].rearrange("p a n -> p (a n)")
            gb = o_ps[E:E + 1, 0:2, :].rearrange("p a n -> p (a n)")

            def g_hi_halves():
                dve.wait_ge(g_done, 1)
                nc.vector.tensor_copy(w_hi[E:P, :], gw).then_inc(w_hi_set, 1)
                dve.wait_ge(g_hi_set, 1)
                nc.vector.tensor_tensor(g_lo, gb, g_hi.bitcast(F32), ALU.subtract).then_inc(w_set, 1)

            def g_lo_half():
                dve.wait_ge(w_hi_set, 3)
                nc.vector.tensor_tensor(w_lo[E:P, :], gw, w_hi[E:P, :].bitcast(F32), ALU.subtract).then_inc(w_set, 1)

            def give_verdict():
                dve.wait_ge(v_pool, 1)
                nc.vector.scalar_tensor_tensor(verdict[0:1, 5:6], verdict[0:1, 0:1], 4.0 * L, verdict[0:1, 4:5], ALU.mult,
                                               ALU.add).then_inc(v_dve, 1)
                dve.wait_ge(v_dve, 2)
                nc.vector.tensor_scalar(verdict[0:1, 6:7], verdict[0:1, 2:3], 0.98, -2 * GAP * EPS, ALU.mult,
                                        ALU.add).then_inc(v_dve, 1)
                dve.wait_ge(v_dve, 3)
                nc.vector.tensor_tensor(verdict[0:1, 7:8], verdict[0:1, 5:6], verdict[0:1, 6:7], ALU.is_le).then_inc(v_dve, 1)
                dve.wait_ge(v_dve, 4)
                scale, shift = (0.0, 1.0) if force_general else (-1.0, 1.0)
                nc.vector.tensor_scalar(flag[:, :], verdict[0:1, 7:8], scale, shift, ALU.mult, ALU.add).then_inc(flag_set, 1)

            def step(g, u, front, mid, back):
                a, b, c = 2 * g + u, 2 * g + u - 1, 2 * (g - 1) + u
                pb = 1 - u
                if not front and not mid:
                    dve.wait_ge(cert_step, 3 * NSEQ)
                    nc.vector.reduce_max(verdict[:, 3:4], cert_max[:, :], AX.X).then_inc(v_dve, 1)

                def keep_et_lo():
                    for odd_tiles in range(2):
                        dve.wait_ge(et_hi_kept, 2 * a + odd_tiles + 1)
                        hi, lo = (tiles_of(et_hl[u][r:r + E, PAD:SPAN], odd_tiles) for r in (0, E))
                        nc.vector.tensor_tensor(lo, pair_bank(et_ps, odd_tiles), hi.bitcast(F32), ALU.subtract).then_inc(et_lo_kept, 1)

                def keep_et_top():
                    dve.wait_ge(et_hi_kept, 2 * a + 2)
                    nc.vector.tensor_copy(et_hh[u][0:E, PAD:SPAN], et_hl[u][0:E, PAD:SPAN].bitcast(F32)).then_inc(et_top_kept, 1)

                def add_shifts(hh):
                    dve.wait_ge(odd_kept, 2 * a + hh + 1)
                    cols = slice(HALF * hh, HALF * (hh + 1))
                    nc.vector.tensor_tensor(hT[u][E * hh:E * hh + E, 0:HALF], conv_ps[0:E, :], odd[0:E, cols],
                                            ALU.add).then_inc(shifts_added, 1)

                def variance(hh):
                    dve.wait_ge(h_ready, b + 1)
                    dve.wait_ge(y_done, 2 * b + hh + 1)
                    y, pairs = y_view(hh), slice(2 * hh, 2 * hh + 2)
                    products = prod[:, 4 * hh:4 * hh + 4, :].rearrange("p (j two) n -> p j two n", two=2)
                    nc.vector.tensor_tensor(products, y[:, :, :, 0:E + 1], in_pairs(h_row)[:, pairs], ALU.mult).then_inc(prod_ready, 1)
                    nc.vector.tensor_scalar(in_pairs(mean_sb[pb][:, :])[:, pairs], y[:, :, :, E + 1], last_moments[:, 1:2],
                                            None, ALU.add)
                    nc.vector.tensor_scalar(in_pairs(lin[:, :])[:, pairs], y[:, :, :, E + 2], last_moments[:, 2:3], None, ALU.add)
                    dve.wait_ge(prod_ready, 2 * b + hh + 1)
                    nc.vector.tensor_reduce(in_pairs(quad[:, :])[:, pairs], products, AX.X, ALU.add).then_inc(quad_ready, 1)

                def scale_h():
                    dve.wait_ge(scal_step, 7 * b + 7)
                    nc.vector.tensor_tensor(bh_row, h_row[:, :, 0:E],
                                            beta[:, :].unsqueeze(2).to_broadcast([P, NT, E]), ALU.mult).then_inc(u_ready, 1)
                    nc.vector.reciprocal(inv_a[:, :], a_sb[pb][:, :]).then_inc(x_step, 1)
                    nc.vector.tensor_copy(x_row[:, :, 2:4], beta[:, :].unsqueeze(2).to_broadcast([P, NT, 2])).then_inc(x_step, 1)
                    dve.wait_ge(x_step, 3 * b + 1)
                    nc.vector.tensor_copy(x_row[:, :, 5:7], inv_a[:, :].unsqueeze(2).to_broadcast([P, NT, 2])).then_inc(x_step, 1)
                    dve.wait_ge(x_step, 3 * b + 2)
                    nc.vector.tensor_tensor(x_row[:, :, 4], beta[:, :], x_row[:, :, 2].bitcast(F32), ALU.subtract)
                    dve.wait_ge(x_step, 3 * b + 3)
                    nc.vector.tensor_tensor(x_row[:, :, 7], inv_a[:, :], x_row[:, :, 5].bitcast(F32),
                                            ALU.subtract).then_inc(x_ready, 1)

                if back:
                    tile_out(c, u, 0)
                if mid and not in_step(1, g, u):
                    variance(0)
                if front:
                    keep_et_lo()
                if back:
                    tile_out(c, u, 1)
                if mid and in_step(1, g, u):
                    variance(0)
                if mid:
                    variance(1)
                    dve.wait_ge(quad_ready, 2 * b + 2)
                    nc.vector.tensor_scalar(var[:, :], quad[:, :], last_moments[:, 0:1], None, ALU.add).then_inc(var_ready, 1)
                if front:
                    keep_et_top()
                if in_step(0, g, u):
                    keep_xbar_rows()
                if back:
                    tile_out(c, u, 2)
                if back:
                    tile_out(c, u, 3)
                if mid:
                    dve.wait_ge(var_ready, b + 1)
                    nc.vector.tensor_scalar(cert[:, :], var[:, :], 2 * GAP + 4 * L, None, ALU.mult).then_inc(cert_step, 1)
                    dve.wait_ge(cert_step, 3 * b + 1)
                    nc.vector.scalar_tensor_tensor(cert[:, :], lin[:, :], -8.0 * L, cert[:, :], ALU.mult,
                                                   ALU.add).then_inc(cert_step, 1)
                    dve.wait_ge(cert_step, 3 * b + 2)
                    nc.vector.tensor_tensor(cert_max[:, :], cert_max[:, :], cert[:, :], ALU.max).then_inc(cert_step, 1)
                if mid:
                    dve.wait_ge(h_hi_kept, b + 1)
                    nc.vector.tensor_tensor(u_lo[pb][0:E, 0:HALF], hT[pb][0:E, 0:HALF], u_hi[pb][0:E, 0:HALF].bitcast(F32), ALU.subtract)
                    nc.vector.tensor_tensor(u_lo[pb][0:E, HALF:T], hT[pb][E:P, 0:HALF], hT[pb][E:P, HALF:T],
                                            ALU.subtract).then_inc(h_lo_kept, 1)
                if in_step(1, g, u):
                    least_gap()
                    weight_halves()
                    scale_h()
                    g_hi_halves()
                if front:
                    add_shifts(0)
                if in_step(1, g, u):
                    g_lo_half()
                if back:
                    tile_out(c, u, 4)
                if mid and not in_step(1, g, u):
                    scale_h()
                if not front and not mid:
                    give_verdict()
                if back:
                    tile_out(c, u, 5)
                if back and not front:
                    tile_out(c, u, 6)
                if mid:
                    for odd_tiles in range(2):
                        dve.wait_ge(hi_kept, 2 * b + odd_tiles + 1)
                        nc.vector.tensor_tensor(tiles_of(u_lo[pb][E:P, :], odd_tiles), pair_bank(sum_ps, odd_tiles),
                                                tiles_of(u_hi[pb][E:P, :], odd_tiles).bitcast(F32), ALU.subtract).then_inc(lo_kept, 1)
                if in_step(0, g, u):
                    keep_xa()
                if front:
                    add_shifts(1)
                if back and front:
                    tile_out(c, u, 6)
                if back:
                    tile_out(c, u, 7)

            def after_step0():
                dve.wait_ge(xa_kept, 1)
                dve.wait_ge(xa_done, 2)
                for n in range(2):
                    nc.vector.tensor_scalar(xaT_sb[:, n, :], mix_ps[:, (E + 1) * n:(E + 1) * (n + 1)], er_w[:, n:n + 1],
                                            None, ALU.mult).then_inc(xa_kept, 1)

            steps(dve, step, after_step0, lambda: None)

            dve.wait_ge(flag_set, 1)
            need = dve.value_load(flag[0:1, 0:1], min_val=0, max_val=1)
            with dve.If(need != 0):
                ab0, ab1 = hT[0][:, :], hT[1][:, :]
                rows = u_rows[:, 0:L]
                spec_x, spec_w = (gathered[n][:, :, :].rearrange("p i n -> p (i n)") for n in range(2))
                left, right = (o_ps[:, n:n + 2, :].rearrange("p a n -> p (a n)") for n in (0, 2))
                lag_row = obuf[:, 0, 0, :]
                LINKS = 26
                with dve.Fori(0, NSEQ * NT) as t:
                    count = [0]

                    def link(ins):
                        count[0] += 1
                        ins.then_inc(g_link, 1)
                        wait_alone(dve, g_link, LINKS * t + count[0], dve_passed)

                    def variance_eps(src, col):
                        for n in range(2):
                            last = nc.vector.bn_stats(g_stats[:, 6 * n:6 * n + 6], src[:, 512 * n:512 * (n + 1)])
                        link(last)
                        link(nc.vector.bn_aggr(g_mv[:, :], g_stats[:, :]))
                        nc.vector.tensor_scalar(g_row[:, col:col + 1], g_mv[:, 1:2], EPS, None, ALU.add).then_inc(g_dve, 1)

                    link(nc.vector.tensor_copy(prod[:, 0, 0:E], h_all[:, bass.ds(E * t, E)]))
                    nc.vector.memset(prod[:, 0, E:E + 1], 1.0).then_inc(g_dve, 1)
                    dve.wait_ge(g_pe, 11 * t + 2)
                    variance_eps(left, 0)
                    link(nc.vector.tensor_copy(g_row[:, 6:7], sum_ps[:, 0:1]))
                    link(nc.vector.tensor_scalar(rows, left, g_row[:, 6:7], None, ALU.add))
                    dve.wait_ge(g_pool, 2 * t + 1)
                    nc.vector.tensor_scalar(ab0, left, g_mv[:, 0:1], g_row[:, 1:2], ALU.subtract, ALU.mult).then_inc(g_dve, 1)
                    dve.wait_ge(g_pe, 11 * t + 5)
                    link(nc.vector.tensor_copy(ab0, right))
                    link(nc.vector.max(g_row[:, 8:16], ab0))
                    link(nc.vector.max_index(g_idx[:, :], g_row[:, 8:16], ab0))
                    nc.vector.tensor_copy(g_row[:, 24:32], g_idx[:, :])
                    link(nc.vector.tensor_scalar(g_row[:, 3:4], g_row[:, 8:9], -1.0, None, ALU.mult))
                    nc.vector.tensor_scalar(g_row[:, 7:8], g_row[:, 8:9], -1.0, None, ALU.mult).then_inc(g_dve, 1)
                    dve.wait_ge(g_act, 7 * t + 4)
                    link(nc.vector.reciprocal(g_row[:, 2:3], g_row[:, 2:3]))
                    link(nc.vector.tensor_scalar(g_row[:, 16:16 + TOPK], g_row[:, 16:16 + TOPK], g_row[:, 2:3], None, ALU.mult))
                    dve.wait_ge(g_table_in, 96 * t + 48)
                    link(nc.vector.tensor_scalar(ab0, lag_row, g_row[:, 24:25], g_row[:, 16:17], ALU.is_equal, ALU.mult))
                    for n in range(1, TOPK):
                        link(nc.vector.tensor_scalar(left, lag_row, g_row[:, 24 + n:25 + n], g_row[:, 16 + n:17 + n],
                                                     ALU.is_equal, ALU.mult))
                        add = nc.vector.tensor_tensor(ab0, ab0, left, ALU.add)
                        if n < TOPK - 1:
                            link(add)
                    add.then_inc(g_dve, 1)
                    dve.wait_ge(g_act, 7 * t + 6)
                    h_ = L // 2
                    xc, xs, wc, ws = spec_x[:, 0:h_], spec_x[:, h_:L], spec_w[:, 0:h_], spec_w[:, h_:L]
                    nc.vector.tensor_tensor(ab0[:, 0:h_], xc, wc, ALU.mult)
                    nc.vector.tensor_tensor(ab0[:, h_:L], xs, wc, ALU.mult)
                    nc.vector.tensor_tensor(left[:, 0:h_], xs, ws, ALU.mult)
                    link(nc.vector.tensor_tensor(left[:, h_:L], xc, ws, ALU.mult))
                    nc.vector.tensor_tensor(ab0[:, 0:h_], ab0[:, 0:h_], left[:, 0:h_], ALU.add)
                    link(nc.vector.tensor_tensor(ab0[:, h_:L], ab0[:, h_:L], left[:, h_:L], ALU.subtract))
                    nc.vector.tensor_tensor(ab0[0:1, 0:P], xc[0:1, 0:P], wc[0:1, 0:P], ALU.mult)
                    nc.vector.tensor_tensor(ab0[0:1, h_:h_ + P], xs[0:1, 0:P], ws[0:1, 0:P], ALU.mult).then_inc(g_dve, 1)
                    dve.wait_ge(g_pe, 11 * t + 8)
                    link(nc.vector.tensor_tensor(rows, rows, left, ALU.add))
                    variance_eps(rows, 4)
                    dve.wait_ge(g_pool, 2 * t + 2)
                    nc.vector.tensor_scalar(ab0, rows, g_mv[:, 0:1], g_row[:, 5:6], ALU.subtract, ALU.mult).then_inc(g_dve, 1)
                    dve.wait_ge(g_pe, 11 * t + 10)
                    for n in range(2):
                        last = nc.vector.tensor_scalar(spec_w[:, P * n:P * (n + 1)], sum_ps[:, P * n:P * (n + 1)],
                                                       er_w[:, n:n + 1], None, ALU.mult)
                    last.then_inc(g_dve, 1)
                    dve.wait_ge(g_pe, 11 * t + 11)
                    nc.vector.tensor_tensor(g_hT[:, :], rows, left, ALU.add).then_inc(g_dve, 1)
                    dve.wait_ge(g_stored, 16 * t + 16)
                    assert count[0] == LINKS, count


        @block.tensor
        def _(pe):
            mm, tr = nc.tensor.matmul, nc.tensor.transpose

            pe.wait_ge(consts_in, 16)
            pe.wait_ge(w2_centred, 1)
            for c in range(KC):
                bank = (sum_ps, mix_ps)[c // 4]
                last = tr(bank[:, (E + 1) * (c % 4):(E + 1) * (c % 4 + 1)], w2c[:, P * c:P * (c + 1)], ident_sb[0:E + 1, 0:E + 1])
            last.then_inc(w2T_done, 1)
            pe.wait_ge(w2T_kept, 2)
            for c in range(KC):
                last = mm(o_ps[0:E + 1, 0, 0:E + 1], w2cT[:, c, :], w2cT[:, c, :], start=(c == 0), stop=(c == KC - 1))
            last.then_inc(mom_done, 1)
            pe.wait_ge(mom_kept, 1)
            pe.wait_ge(hbar_set, 1)
            pe.wait_ge(ones_set, 1)
            mm(o_ps[0:E + 1, 1, 0:1], moments[:, 0:E + 1], hbar[:, 0:1], start=True, stop=True).then_inc(mom_done, 1)
            pe.wait_ge(mom_kept, 2)
            mm(o_ps[:, 2, 0:1], hbar[:, :], moments[:, E + 2:E + 3], start=True, stop=True)
            mm(o_ps[:, 2, 1:4], hbar[E:E + 1, :], moments[E:E + 1, E:E + 3], start=True, stop=True).then_inc(mom_done, 1)

            def conv(u, col, width):
                for m in range(J // 2):
                    mm(conv_ps[:, 0:width], shift_hi[:, 2 * m:2 * m + 2, :], et_hl[u][:, col - 2 * m:col - 2 * m + width],
                       start=(m == 0), stop=False)
                for m in range(J // 4):
                    last = mm(conv_ps[:, 0:width], shift_lo[:, 2 * m:2 * m + 2, :],
                              et_hh[u][:, col - 2 * m:col - 2 * m + width], start=False, stop=(m == J // 4 - 1))
                return last

            tr(o_ps[:, 3, 0:E + 1], hbar[:, :], ident_sb[0:E + 1, 0:E + 1]).then_inc(mom_done, 1)

            def padding_conv():
                pe.wait_ge(shift_set, 2)
                pe.wait_ge(pads_set, 2)
                conv(0, J - 2, 2).then_inc(pad_conv_done, 1)

            def xbar_by_rows():
                pe.wait_ge(mom_kept, 4)
                tr(o_ps[0:KC, 0, 0:P], xbar_col[:, :], ident_sb[:, :]).then_inc(mom_done, 1)

            def xa_product():
                pe.wait_ge(aT_in, 16)
                for c in range(KC):
                    last = mm(sum_ps[0:E + 1, 0:ER], w2cT[:, c, :], aT_sb[:, c, :], start=(c == 0), stop=(c == KC - 1))
                last.then_inc(xa_done, 1)

            def weight_products(first, end):
                pe.wait_ge(mom_kept, 5)
                for c in range(first, end):
                    if c % 2 == 0:
                        pe.wait_ge(wT_in[c // 2], 16)
                    for n in range(2):
                        mm(o_ps[0:E + 1, n, :], w2cT[:, c, :], wT_sb[:, c, 512 * n:512 * (n + 1)], start=(c == 0), stop=False)

            def low_rank_products():
                pe.wait_ge(bfT_in, 16)
                for e in range(2):
                    for n in range(2):
                        last = mm(o_ps[0:E + 1, n, :], xaT_sb[:, e, :], bfT_sb[:, e, 512 * n:512 * (n + 1)], start=False, stop=(e == 1))
                last.then_inc(g_done, 1)

            def xbar_correlation():
                pe.wait_ge(hankel_in, 32)
                pe.wait_ge(xbar_step, 2)
                for c in range(KC):
                    mm(o_ps[0:1, 2, :], xbar_col_r[:, c:c + 1], hankel(c), start=(c == 0), stop=(c == KC - 1))
                for c in range(KC):
                    last = mm(o_ps[0:1, 3, 0:1], xbar_col[:, c:c + 1], xbar_col[:, c:c + 1], start=(c == 0), stop=(c == KC - 1))
                last.then_inc(acf_done, 1)

            def step(g, u, front, mid, back):
                a, b, c = 2 * g + u, 2 * g + u - 1, 2 * (g - 1) + u
                pb = 1 - u

                def tile_product(i):
                    if i == 0:
                        pe.wait_ge(h_hi_kept, c + 1)
                        pe.wait_ge(h_lo_kept, c + 1)
                        pe.wait_ge(hi_kept, 2 * c + 2)
                        pe.wait_ge(lo_kept, 2 * c + 2)
                        pe.wait_ge(xt_kept, c + 1)
                    if i == 1 and in_step(2, g, u):
                        pe.wait_ge(rows_in, 48)
                    ge(pe, oa_kept, NT * c + i - 1)
                    ge(pe, ov_kept, NT * c + i - 1)
                    cols = slice(P * i, P * (i + 1))
                    factors = ((u_hi[u][:, cols], w_hi), (u_lo[u][:, cols], w_hi), (u_hi[u][:, cols], w_lo),
                               (xT[u][:, P * (i // 4):P * (i // 4 + 1)], extra[i % 4]))
                    for n in range(2):
                        for f, (lhsT, rhs) in enumerate(factors):
                            last = mm(o_ps[:, 2 * (i % 2) + n, :], lhsT, rhs[:, 512 * n:512 * (n + 1)],
                                      start=(f == 0), stop=(f == len(factors) - 1))
                    last.then_inc(o_done, 1)

                def transpose_rows():
                    pe.wait_ge(rows_gathered[u], 16 * NT * (g + 1))
                    ge(pe, et_lo_kept, 2 * a)
                    ge(pe, xt_kept, a - 1)
                    for j in range(NT // 2):
                        last = tr(et_ps[:, P * j:P * (j + 1)],
                                  gathered[u][:, 2 * j:2 * j + 2, :].rearrange("p i e -> p (i e)"), ident_sb[:, :])
                    last.then_inc(et_done, 1)

                def transpose_h():
                    ge(pe, hi_kept, 2 * b)
                    ge(pe, lo_kept, 2 * b)
                    pe.wait_ge(tanh_done, 2 * b + 2)
                    for j in range(NT // 2):
                        last = tr(sum_ps[:, P * j:P * (j + 1)], hT[pb][:, P * j:P * (j + 1)], ident_sb[:, :])
                    last.then_inc(h_done, 1)

                def moments_of(hh):
                    if hh == 0 and in_step(1, g, u):
                        pe.wait_ge(xa_kept, 4)
                    elif hh == 1:
                        pe.wait_ge(h_ready, b + 1)
                    bank, width = (mix_ps, sum_ps)[hh], 2 * (E + 3)
                    for n in range(2):
                        col = P * (2 * hh + n)
                        last = mm(bank[:, width * n:width * (n + 1)], hT[pb][:, col:col + P], moments_two[:, :], start=True, stop=True)
                    last.then_inc(y_done, 1)

                def conv_half(hh):
                    if in_step(0, g, u):
                        pe.wait_ge(pad_conv_kept, 1)
                    if hh == 0:
                        pe.wait_ge(et_lo_kept, 2 * a + 2)
                        pe.wait_ge(et_top_kept, a + 1)
                        pe.wait_ge(et_back_kept, a + 1)
                    ge(pe, shifts_added, 2 * a + hh)
                    conv(u, PAD + HALF * hh, HALF).then_inc(conv_done, 1)

                if back:
                    tile_product(0)
                if mid and not in_step(1, g, u):
                    transpose_h()
                    moments_of(0)
                if front:
                    transpose_rows()
                if in_step(0, g, u):
                    xbar_by_rows()
                    padding_conv()
                if in_step(1, g, u):
                    weight_products(0, 2)
                    transpose_h()
                    xbar_correlation()
                    moments_of(0)
                if back:
                    tile_product(1)
                if mid:
                    moments_of(1)
                if back:
                    tile_product(2)
                if back:
                    tile_product(3)
                if in_step(1, g, u):
                    weight_products(2, KC)
                    low_rank_products()
                if front:
                    conv_half(0)
                if in_step(0, g, u):
                    xa_product()
                if back:
                    tile_product(4)
                    tile_product(5)
                if back and not front:
                    tile_product(6)
                if mid:
                    pe.wait_ge(u_ready, b + 1)
                    for j in range(NT // 2):
                        last = tr(sum_ps[:, P * j:P * (j + 1)], bh_row[:, 2 * j:2 * j + 2, :].rearrange("p i e -> p (i e)"),
                                  ident_sb[:, :])
                    last.then_inc(ut_done, 1)
                    pe.wait_ge(x_ready, b + 1)
                    ge(pe, et_lo_kept, 2 * (a + front))
                    for hh in range(2):
                        last = tr(et_ps[:, P * hh:P * (hh + 1)],
                                  x_row[:, 4 * hh:4 * hh + 4, :].bitcast(F32).rearrange("p i x -> p (i x)"), ident_sb[:, :])
                    last.then_inc(xt_done, 1)
                if front:
                    conv_half(1)
                if back and front:
                    tile_product(6)
                if back:
                    tile_product(7)

            def after_step0():
                pe.wait_ge(xa_kept, 2)
                for n in range(2):
                    last = tr(mix_ps[:, (E + 1) * n:(E + 1) * (n + 1)], xa_sb[:, P * n:P * (n + 1)], ident_sb[0:E + 1, 0:E + 1])
                last.then_inc(xa_done, 1)

            def after_step1():
                pe.wait_ge(w_set, 5)
                pe.wait_ge(acf_kept, 2)
                pe.wait_ge(row0_in, 16 * NX)

            pe.wait_ge(blocks_set, 2)
            steps(pe, step, after_step0, after_step1)

            pe.wait_ge(flag_set, 1)
            need = pe.value_load(flag[0:1, 0:1], min_val=0, max_val=1)
            with pe.If(need != 0):
                ab0, ab1 = hT[0][:, :], hT[1][:, :]
                spec_w = gathered[1][:, :, :].rearrange("p i n -> p (i n)")
                left, right = (o_ps[:, n:n + 2, :].rearrange("p a n -> p (a n)") for n in (0, 2))
                table = obuf[:, :, :, :].rearrange("p a b n -> p (a b) n")

                def transpose_all():
                    for c in range(KC):
                        last = tr(right[:, P * c:P * (c + 1)], ab0[:, P * c:P * (c + 1)], ident_sb[:, :])
                    last.then_inc(g_pe, 1)

                def spectrum():
                    for m in range(KC):
                        for c in range(KC):
                            last = mm(left[:, P * m:P * (m + 1)], table[:, c, P * m:P * (m + 1)], ab1[:, P * c:P * (c + 1)],
                                      start=(c == 0), stop=(c == KC - 1))
                    last.then_inc(g_pe, 1)

                def rows_from(dst, lhsT):
                    for n in range(2):
                        for c in range(KC):
                            last = mm(dst[:, 512 * n:512 * (n + 1)], lhsT[:, P * c:P * (c + 1)], table[:, c, 512 * n:512 * (n + 1)],
                                      start=(c == 0), stop=(c == KC - 1))
                    last.then_inc(g_pe, 1)

                with pe.Fori(0, NSEQ * NT) as t:
                    pe.wait_ge(g_dve, 10 * t + 1)
                    tr(mix_ps[0:E + 1, 0:P], prod[:, 0, :], ident_sb[:, :]).then_inc(g_pe, 1)
                    pe.wait_ge(g_act, 7 * t + 1)
                    for n in range(2):
                        mm(left[:, 512 * n:512 * (n + 1)], g_hT[0:E + 1, 0:P], w2c[:, 512 * n:512 * (n + 1)], start=True, stop=True)
                    mm(sum_ps[:, 0:1], g_hT[0:E + 1, 0:P], w2mean[:, :], start=True, stop=True).then_inc(g_pe, 1)
                    pe.wait_ge(g_dve, 10 * t + 3)
                    transpose_all()
                    pe.wait_ge(g_act, 7 * t + 2)
                    pe.wait_ge(g_table_in, 96 * t + 16)
                    spectrum()
                    pe.wait_ge(g_act, 7 * t + 3)
                    pe.wait_ge(g_table_in, 96 * t + 32)
                    rows_from(right, spec_w)
                    pe.wait_ge(g_dve, 10 * t + 5)
                    transpose_all()
                    pe.wait_ge(g_act, 7 * t + 5)
                    pe.wait_ge(g_table_in, 96 * t + 64)
                    spectrum()
                    pe.wait_ge(g_dve, 10 * t + 6)
                    pe.wait_ge(g_table_in, 96 * t + 80)
                    rows_from(left, ab0)
                    pe.wait_ge(g_dve, 10 * t + 8)
                    transpose_all()
                    pe.wait_ge(g_act, 7 * t + 7)
                    for e in range(2):
                        for c in range(KC):
                            last = mm(sum_ps[:, P * e:P * (e + 1)], aT_sb[:, c, P * e:P * (e + 1)], ab1[:, P * c:P * (c + 1)],
                                      start=(c == 0), stop=(c == KC - 1))
                    last.then_inc(g_pe, 1)
                    pe.wait_ge(g_dve, 10 * t + 9)
                    pe.wait_ge(g_table_in, 96 * t + 96)
                    for n in range(2):
                        cols = slice(512 * n, 512 * (n + 1))
                        for c in range(KC):
                            mm(left[:, cols], ab1[:, P * c:P * (c + 1)], table[:, c, cols], start=(c == 0), stop=False)
                        for e in range(2):
                            mm(left[:, cols], spec_w[:, P * e:P * (e + 1)], bfT_sb[:, e, cols], start=False, stop=False)
                        last = mm(left[:, cols], g_ones[:, :], bias_row[:, cols], start=False, stop=True)
                    last.then_inc(g_pe, 1)



def kernel(**inputs):
    import concourse.bacc as bacc
    from concourse.bass_utils import run_bass_kernel_spmd

    x, w = inputs["x"], inputs["L0_ffn_W"]
    a, bf = inputs["L0_ffn_A"], inputs["L0_ffn_Bf"]
    by_rank = lambda v: np.ascontiguousarray(np.repeat(v, R).reshape(2, P).T)
    half = L // 2
    freq = np.concatenate([np.arange(half), np.arange(half)])
    freq[half] = half
    turn = np.outer(np.arange(L), freq) % L
    cosine = np.cos(2 * np.pi * np.minimum(turn, L - turn) / L)
    sine = np.sin(2 * np.pi * turn / L)
    dft = np.concatenate([cosine[:, :half + 1], sine[:, half + 1:]], 1)
    weight = np.where((np.arange(L) == 0) | (np.arange(L) == half), 1.0, 2.0) / L
    arrays = {
        "ids": np.ascontiguousarray(np.asarray(x).reshape(NSEQ * NT, P).T),
        "wte": inputs["L0_tok_wte"], "w1": inputs["L0_tok_w1"], "b1": inputs["L0_tok_b1"].reshape(E, 1),
        "w2": inputs["L0_tok_w2"], "b2": inputs["L0_tok_b2"].reshape(1, L),
        "wT": np.ascontiguousarray(w.T), "bias": inputs["L0_ffn_bias"].reshape(1, L),
        "aT": np.ascontiguousarray(a.reshape(ER, L).T),
        "bfT": np.ascontiguousarray(bf.transpose(0, 2, 1).reshape(ER, L)),
        "coeffs": by_rank(inputs["L0_ffn_coeffs"]), "scales": by_rank(inputs["L0_ffn_scales"]),
        "ident": np.eye(P, dtype=np.float32),
        "dft": dft.astype(np.float32),
        "idft": np.ascontiguousarray((dft * weight).T.astype(np.float32)),
        "acf": np.ascontiguousarray((cosine * weight).T.astype(np.float32)),
        "lags": np.tile(np.arange(L, dtype=np.float32), (P, 1)),
    }
    arrays = {n: np.ascontiguousarray(v) for n, v in arrays.items()}
    nc = bacc.Bacc("TRN2", target_bir_lowering=False, num_devices=1)
    args = {n: nc.dram_tensor(f"in_{n}", v.shape, mybir.dt.from_np(v.dtype), kind="ExternalInput").ap()
            for n, v in arrays.items()}
    out = nc.dram_tensor("out", (NSEQ, T, L), F32, kind="ExternalOutput").ap()
    tower_kernel(nc, out=out, **args)
    res = run_bass_kernel_spmd(nc, [{f"in_{n}": v for n, v in arrays.items()}], core_ids=[0])
    return res.results[0]["out"]
```
